# Optimizing a Trainium2 kernel written in Bass

```python
import numpy as np
import jax
import jax.numpy as jnp

def _softmax(x, axis=-1):
    return jax.nn.softmax(x, axis=axis)

def _gelu(x):
    return jax.nn.gelu(x, approximate=True)

def _silu(x):
    return jax.nn.silu(x)

def _sigmoid(x):
    return jax.nn.sigmoid(x)

def _layernorm(x, axis=-1, eps=1e-05):
    m = jnp.mean(x, axis=axis, keepdims=True)
    v = jnp.var(x, axis=axis, keepdims=True)
    return (x - m) / jnp.sqrt(v + eps)

def _scatter_add(tgt, idx, src, axis=0):
    return tgt.at[idx].add(src)

def _segment_sum(src, seg, n):
    return jax.ops.segment_sum(src, seg, n)
kernel_name = 'mk_seq_postln_d1_jaxref_r8_7c0e26'

def setup_inputs(seed: int=0):
    np.random.seed(seed)
    _w = jnp.asarray

    def _L0_attn_setup():
        import jax, jax.numpy as jnp
        import numpy as np
        B, T, D = (1, 256, 512)
        H, G = (32, 8)
        HD = D // H
        REP = H // G
        KV_DIM = 2 * HD * G
        key = jax.random.key(seed)
        k0, k1, k2, k3 = jax.random.split(key, 4)
        x = jax.random.normal(k0, (B, T, D), dtype=jnp.float32)
        Wq = jax.random.normal(k1, (D, D), dtype=jnp.float32) * 0.02
        Wkv = jax.random.normal(k2, (D, KV_DIM), dtype=jnp.float32) * 0.02
        Wo = jax.random.normal(k3, (D, D), dtype=jnp.float32) * 0.02
        bo = jnp.zeros((D,), dtype=jnp.float32)
        return {'x': x, 'Wq': Wq, 'Wkv': Wkv, 'Wo': Wo, 'bo': bo}
    _L0_attn_in = _L0_attn_setup()

    def _L0_ffn_setup():
        import jax, jax.numpy as jnp
        import numpy as np
        B_, S, D_IN, D_OUT = (4, 256, 512, 512)
        N, RANK, ALPHA = (8, 16, 32)
        SCALE = ALPHA / RANK
        key = jax.random.key(seed)
        kx, ka, kb, kw, kbias = jax.random.split(key, 5)
        x = jax.random.normal(kx, (B_, S, D_IN), dtype=jnp.float32)
        lora_A = jax.random.normal(ka, (N, RANK, D_IN), dtype=jnp.float32) * (1.0 / np.sqrt(D_IN))
        lora_B = jax.random.normal(kb, (N, D_OUT, RANK), dtype=jnp.float32) * (1.0 / np.sqrt(RANK))
        W = jax.random.normal(kw, (D_OUT, D_IN), dtype=jnp.float32) * (1.0 / np.sqrt(D_IN))
        bias = jax.random.normal(kbias, (D_OUT,), dtype=jnp.float32) * 0.01
        lora_weights = jnp.full((N,), 1.0 / N, dtype=jnp.float32)
        return {'x': x, 'lora_A': lora_A, 'lora_B': lora_B, 'W': W, 'bias': bias, 'lora_weights': lora_weights}
    _L0_ffn_in = _L0_ffn_setup()
    _d = {'L0_attn_x': _L0_attn_in['x'], 'L0_attn_Wq': _L0_attn_in['Wq'], 'L0_attn_Wkv': _L0_attn_in['Wkv'], 'L0_attn_Wo': _L0_attn_in['Wo'], 'L0_attn_bo': _L0_attn_in['bo'], 'L0_ffn_lora_A': _L0_ffn_in['lora_A'], 'L0_ffn_lora_B': _L0_ffn_in['lora_B'], 'L0_ffn_W': _L0_ffn_in['W'], 'L0_ffn_bias': _L0_ffn_in['bias'], 'L0_ffn_lora_weights': _L0_ffn_in['lora_weights']}
    _x0 = _d['L0_attn_x']
    _d['L0_attn_x'] = jax.random.normal(jax.random.fold_in(jax.random.key(seed), 1), (1, 1024, 512), dtype=_x0.dtype)
    del _x0
    return _d

def reference(L0_attn_x, L0_attn_Wq, L0_attn_Wkv, L0_attn_Wo, L0_attn_bo, L0_ffn_lora_A, L0_ffn_lora_B, L0_ffn_W, L0_ffn_bias, L0_ffn_lora_weights):

    def _L0_attn_ref(x, Wq, Wkv, Wo, bo):
        import jax, jax.numpy as jnp
        import numpy as np
        B, T, D = (1, 256, 512)
        H, G = (32, 8)
        HD = D // H
        REP = H // G
        KV_DIM = 2 * HD * G
        b, t, d = x.shape
        q = jnp.dot(x, Wq).reshape(b, t, H, HD).transpose(0, 2, 1, 3)
        kv = jnp.dot(x, Wkv).reshape(b, t, G, 2, HD).transpose(2, 3, 0, 1, 4)
        k, v = (kv[:, 0], kv[:, 1])
        k = jnp.broadcast_to(k[:, :, None], (G, b, REP, t, HD)).reshape(b, H, t, HD)
        v = jnp.broadcast_to(v[:, :, None], (G, b, REP, t, HD)).reshape(b, H, t, HD)
        scores = jnp.einsum('bhqd,bhkd->bhqk', q, k)
        causal = jnp.triu(jnp.ones((t, t), dtype=bool), 1)
        scores = jnp.where(causal[None, None], -jnp.inf, scores)
        weights = jax.nn.softmax(scores * (1.0 / HD ** 0.5), axis=-1)
        ctx = jnp.einsum('bhqk,bhkd->bhqd', weights, v)
        ctx = ctx.transpose(0, 2, 1, 3).reshape(b, t, d)
        return jnp.dot(ctx, Wo) + bo

    def _L0_ffn_ref(x, lora_A, lora_B, W, bias, lora_weights):
        import jax, jax.numpy as jnp
        import numpy as np
        B_, S, D_IN, D_OUT = (4, 256, 512, 512)
        N, RANK, ALPHA = (8, 16, 32)
        SCALE = ALPHA / RANK
        h = jnp.einsum('bsd,nrd->nbsr', x, lora_A)
        coef = (SCALE * lora_weights)[:, None, None]
        lora_out = jnp.einsum('nbsr,nor->bso', h, lora_B * coef)
        base = jnp.einsum('bsd,od->bso', x, W) + bias
        return base + lora_out
    x = L0_attn_x
    x = _layernorm(x + _L0_attn_ref(x, L0_attn_Wq, L0_attn_Wkv, L0_attn_Wo, L0_attn_bo), axis=-1)
    x = _layernorm(x + _L0_ffn_ref(x, L0_ffn_lora_A, L0_ffn_lora_B, L0_ffn_W, L0_ffn_bias, L0_ffn_lora_weights), axis=-1)
    return x

_drawn_inputs = setup_inputs


def setup_inputs(seed=0):
    import zlib

    import numpy as np

    out = dict(_drawn_inputs(seed))
    spreads = {'L0_attn_bo': (0.0, 0.1), 'L0_ffn_lora_weights': (0.125, 0.2)}
    factors = {'L0_attn_Wq': 8.0, 'L0_attn_Wkv': 3.362, 'L0_attn_Wo': 3.759, 'L0_ffn_bias': 8.0}
    for name, (base, spread) in spreads.items():
        noise = np.random.default_rng([zlib.crc32(name.encode()), seed]).standard_normal(out[name].shape)
        drawn = base * np.exp(spread * noise) if base else spread * noise
        out[name] = jnp.asarray(drawn.astype(out[name].dtype))
    for name, factor in factors.items():
        out[name] = (out[name] * factor).astype(out[name].dtype)
    return out
```

```python
import numpy as np
import concourse.bass as bass
from concourse import mybir
from contextlib import ExitStack

F32 = mybir.dt.float32
F32R = mybir.dt.float32r
BF16 = mybir.dt.bfloat16
ACT = mybir.ActivationFunctionType
ALU = mybir.AluOpType
AX = mybir.AxisListType.X

P = 128
LOWEST = -3.0e38
EPS = 1e-5
ONE_ONE = float(np.array([0x3F803F80], np.uint32).view(np.float32)[0])
ALPHA = 32


def postln_kernel(nc, x, wq, wkv, wo, bo, lora_a, lora_b, w, bias, lora_w, out):
    _, T, D = x.shape
    N_LORA, RANK, _ = lora_a.shape
    HD = 16
    H = D // HD
    G = wkv.shape[1] // (2 * HD)
    REP = H // G
    NC = D // P
    NT = T // P
    HT = T // 2
    TB = HT // P
    KD = G * HD
    SCALE = 1.0 / HD ** 0.5
    LORA_SCALE = ALPHA / RANK
    assert KD == P and N_LORA * RANK == P and D == HT == 512 and REP == 4

    NPART = 3
    ROWS = 6 * HD
    NROW = ROWS + NPART

    NU = 2 * G
    CYCLES = [(u, kb) for u in range(NU) for kb in range(TB * (1 + u // G))]
    FIRST = [CYCLES.index((u, 0)) for u in range(NU)]
    NCYC = len(CYCLES)
    LEAD = 4
    SLOTS = 6
    AHEAD = 5
    NP_BUF = 3

    def half_of(u):
        return u // G

    def items_due(c):
        if c + LEAD >= NCYC:
            return 16 * NU
        v, o = CYCLES[c + LEAD]
        return min(16 * NU, 16 * (v + 1) + 16 * o // (TB * (1 + half_of(v))))

    def chunks_before(i):
        return i if i <= 16 * G else 2 * i - 16 * G

    def item(i):
        u, k = divmod(i, 16)
        return u, k // REP, k % REP

    def rows_cycle(u):
        return FIRST[u] - LEAD + 1 if u else -1

    ctx = ExitStack()
    with ctx:
        def sb(name, shape, dt=F32):
            return ctx.enter_context(nc.sbuf_tensor(name, shape, dt))

        def sem(name):
            return ctx.enter_context(nc.semaphore(name))

        X = sb("X", [P, NT, D])
        RAW = sb("RAW", [P, NU, HT])
        xT = RAW[:, 0:G, :].rearrange("p a b -> p (a b)").rearrange("p (c t) -> p c t", c=NC)
        wq_raw = RAW[:, G:G + 4, :]
        wo_raw = RAW[:, G + 4:G + 8, :]
        XT = sb("XT", [P, 2, NC, T], F32R)
        WE = XT[:, 0, :, 0:D]
        WEL = XT[:, 1, :, 0:D]
        CT = XT[:, :, :, D:D + 2 * P].rearrange("p a c (b t) -> p b a c t", b=2)
        X1T = XT[:, :, :, D + 2 * P:D + 4 * P].rearrange("p a c (b t) -> p b a c t", b=2)
        WQ = sb("WQ", [P, 2, NC, D + KD], F32R)
        wkv_raw = sb("wkv_raw", [P, NC, 2 * KD])
        wkv_v = wkv_raw[:, :, :].rearrange("p c (g two d) -> p c two g d", two=2, d=HD)
        coef = sb("coef", [P, N_LORA])
        bo_bc = sb("bo_bc", [P, D])
        bias_bc = sb("bias_bc", [P, D])
        QS = sb("QS", [P, SLOTS, REP, HT], BF16)
        KS = sb("KS", [P, G, T], BF16)
        VX = sb("VX", [P, NT, G, 2 * HD])
        PB = sb("PB", [P, NP_BUF, REP, HT])
        PB_flat = PB[:, :, :, :].rearrange("p a b c -> p (a b c)")
        parts = sb("parts", [P, 2, NPART, HT], BF16)
        rest = sb("rest", [P, 2, HT])
        ident = sb("ident", [P, P])
        ident_bf = sb("ident_bf", [P, P], BF16)
        mask = sb("mask", [P, P])
        scrap = sb("scrap", [P, 2, P])
        MX = sb("MX", [P, 2, 16, 3])
        NM = sb("NM", [P, 2, 16])
        NM2 = sb("NM2", [P, 2, 16])
        NMP = sb("NMP", [P, 2, TB, NPART, REP], BF16)
        NMR = sb("NMR", [P, 2, HT], BF16)
        stats = sb("stats", [P, 4, 6])
        mv = sb("mv", [P, 4, 2])
        std = sb("std", [P, 4])
        rstd = sb("rstd", [P, 4])
        rec = sb("rec", [P, 2, H])

        w_raw = PB_flat[:, 0:NC * D].rearrange("p (c d) -> p c d", c=NC)

        def tile_c(n):
            return PB_flat[:, n * D:(n + 1) * D]
        a_raw, bT = tile_c(4), tile_c(5)
        b_raw = tile_c(6).rearrange("p (c n r) -> p c n r", c=NC, n=N_LORA)
        CTX = [tile_c(0), tile_c(1)]
        Y1 = [tile_c(2), tile_c(3)]
        X1 = [tile_c(4), tile_c(5), tile_c(6)]
        Y2 = [tile_c(7), tile_c(8)]
        OUT = [tile_c(9), tile_c(10)]
        X1B = [tile_c(11), rest[:, 0, :]]

        PS = ctx.enter_context(nc.psum_tensor("PS", [P, 8, 512], F32))
        MAX0, ST0, PV_BANK, MISC = 0, 2, 6, 7

        scr_q = nc.dram_tensor("scr_q", (NPART, D, T), BF16).ap()
        scr_k = nc.dram_tensor("scr_k", (NPART, KD, T), BF16).ap()
        scr_m = nc.dram_tensor("scr_m", (NU, NPART * REP, HT), BF16).ap()

        x_in = [sem(f"x_in{h}") for h in range(2)]
        wkv_in, wq_in, ab_in, w_in, wo_in, bo_in = (sem(n) for n in (
            "wkv_in", "wq_in", "ab_in", "w_in", "wo_in", "bo_in"))
        consts = sem("consts")
        job_done = sem("job_done")
        job_freed = sem("job_freed")
        act_copied = sem("act_copied")
        wk_split, wq_split = sem("wk_split"), sem("wq_split")
        b_scaled, wo_split = sem("b_scaled"), sem("wo_split")
        parts_ready = sem("parts_ready")
        parts_out = [sem(f"parts_out{b}") for b in range(2)]
        ks_in = [sem(f"ks_in{h}") for h in range(2)]
        qs_in = [sem(f"qs_in{s}") for s in range(SLOTS)]
        max_scores = sem("max_scores")
        max_read = sem("max_read")
        nm_parts = sem("nm_parts")
        nm_turned = sem("nm_turned")
        nm_rows = sem("nm_rows")
        nm_out = sem("nm_out")
        nm_in = sem("nm_in")
        scores = sem("scores")
        probs = sem("probs")
        masked = sem("masked")
        pv_done = sem("pv_done")
        raw_out = sem("raw_out")
        xr_ready = sem("xr_ready")
        dve_step, pool_step = sem("dve_step"), sem("pool_step")
        t1_done, t2_done, wo_done, t3_done, ffn_done = (sem(n) for n in (
            "t1_done", "t2_done", "wo_done", "t3_done", "ffn_done"))
        ctx_ready, ct_hi, ct_ready = sem("ctx_ready"), sem("ct_hi"), sem("ct_ready")
        ln_var, ln_std = sem("ln_var"), sem("ln_std")
        y1_read, x1_ready, x1_hi, x1t_ready = (sem(n) for n in ("y1_read", "x1_ready", "x1_hi", "x1t_ready"))
        x1b_ready, y2_read, out_ready = sem("x1b_ready"), sem("y2_read"), sem("out_ready")
        out_done = [sem(f"out_done{b}") for b in range(2)]

        JOBS = [("xT", h, c) for h in range(2) for c in range(NC)]
        for h in range(2):
            JOBS += [("V", h, 0), ("K", h, 0)] + [("Q", h, c) for c in range(NC)]
        JOBS += [("bT", 0, 0)] + [("WE", 0, c) for c in range(NC)]
        JOB = {job: n for n, job in enumerate(JOBS)}
        NJOB = len(JOBS)
        RING = 6
        PROJ = [j for j in JOBS if j[0] in "KQ"]
        COPIED = [j for j in JOBS if j[0] != "V" and j[0] != "bT"]
        EARLY = JOB[("V", 1, 0)]
        PER_JOB = -(-items_due(0) // (NJOB - 1 - EARLY))

        def job_bank(n):
            return PS[:, 2 + n % RING, :]

        def early_items(n):
            return 0 if n < EARLY else min(items_due(0), PER_JOB * (n - EARLY + 1))

        x_v = x.rearrange("a (h b p) d -> (a h) p b d", h=2, p=P)
        out_v = out.rearrange("a (b p) d -> (a b) p d", p=P)

        block = ctx.enter_context(nc.Block())

        @block.sync
        def _(sp):
            sp.dma_start(X[:, 0:TB, :], x_v[0]).then_inc(x_in[0], 16)
            sp.dma_start(wkv_raw[:, :, :], wkv.rearrange("(c p) n -> p c n", p=P)).then_inc(wkv_in, 16)
            sp.dma_start(wq_raw, wq.rearrange("(c p) n -> p c n", p=P)).then_inc(wq_in, 16)
            sp.dma_start(X[:, TB:NT, :], x_v[1]).then_inc(x_in[1], 16)
            sp.dma_start(w_raw[:, :, :], w.rearrange("(c p) n -> p c n", p=P)).then_inc(w_in, 16)
            sp.dma_start(a_raw[:, :], lora_a.rearrange("n r d -> (n r) d")).then_inc(ab_in, 16)
            for c in range(NC):
                sp.dma_start(b_raw[:, c, :, :], lora_b[:, c * P:(c + 1) * P, :].rearrange("n p r -> p n r"))\
                    .then_inc(ab_in, 16)
            sp.dma_start(coef[:, :], lora_w.partition_broadcast(P)).then_inc(ab_in, 16)
            sp.dma_start(wo_raw, wo.rearrange("(c p) n -> p c n", p=P)).then_inc(wo_in, 16)
            sp.dma_start(bo_bc[:, :], bo.partition_broadcast(P)).then_inc(bo_in, 16)
            sp.dma_start(bias_bc[:, :], bias.partition_broadcast(P)).then_inc(bo_in, 16)

            def parts_to_dram(n):
                kind, h, c = PROJ[n]
                sp.wait_ge(parts_ready, n + 1)
                dst = scr_k if kind == "K" else scr_q[:, c * P:(c + 1) * P, :]
                sp.dma_start(dst[:, :, h * HT:(h + 1) * HT].rearrange("a p t -> p a t"),
                             parts[:, n % 2, :, :]).then_inc(parts_out[n % 2], 16)

            def parts_landed(n):
                sp.wait_ge(parts_out[n % 2], 16 * (n // 2 + 1))

            def load_keys(h):
                parts_landed(PROJ.index(("K", h, 0)))
                src = scr_k[:, :, h * HT:(h + 1) * HT].rearrange("a (g d) t -> a d g t", d=HD)
                row = 0
                for run in (3, 2, 1):
                    for a in range(run):
                        sp.dma_start(KS[row:row + HD, :, h * HT:(h + 1) * HT], src[a]).then_inc(ks_in[h], 16)
                        row += HD

            def load_queries(u):
                h, g = divmod(u, G)
                slot = u % SLOTS
                if u >= SLOTS:
                    sp.wait_ge(scores, 2 * FIRST[u - SLOTS + 1])
                parts_landed(PROJ.index(("Q", h, g // 2)))
                row = 0
                for a, copies in enumerate((3, 2, 1)):
                    src = scr_q[a, g * REP * HD:(g + 1) * REP * HD, h * HT:(h + 1) * HT]\
                        .rearrange("(j d) t -> d j t", d=HD)
                    for _ in range(copies):
                        sp.dma_start(QS[row:row + HD, slot, :, :], src).then_inc(qs_in[slot], 16)
                        row += HD

            def move_maxima(u):
                sp.wait_ge(nm_rows, u + 1)
                sp.dma_start(scr_m[u], NMR[0:NPART * REP, u % 2, :]).then_inc(nm_out, 16)
                sp.wait_ge(nm_out, 16 * (u + 1))
                sp.dma_start(QS[ROWS:NROW, u % SLOTS, :, :],
                             scr_m[u].rearrange("(a j) t -> a j t", a=NPART)).then_inc(nm_in, 16)
                sp.wait_ge(nm_in, 16 * (u + 1))

            loaded = 0
            for n, (kind, h, c) in enumerate(PROJ):
                parts_to_dram(n)
                if n and PROJ[n - 1][0] == "K":
                    load_keys(PROJ[n - 1][1])
                if n and PROJ[n - 1][0] == "Q" and PROJ[n - 1][1] == 0:
                    for u in (2 * PROJ[n - 1][2], 2 * PROJ[n - 1][2] + 1):
                        if u < SLOTS:
                            load_queries(u)
                            loaded = u + 1
            for u in range(NU):
                move_maxima(u)
                if u + AHEAD < NU and u + AHEAD >= loaded:
                    load_queries(u + AHEAD)
            for b in range(NT):
                sp.wait_ge(out_ready, b + 1)
                sp.dma_start(out_v[b], OUT[b % 2]).then_inc(out_done[b % 2], 16)
            for s in range(2):
                sp.wait_ge(out_done[s], 16 * (NT // 2))

        @block.gpsimd
        def _(pool):
            step = [0]

            def link(ins):
                step[0] += 1
                ins.then_inc(pool_step, 1)
                pool.wait_ge(pool_step, step[0])

            def constant(ins, n):
                ins.then_inc(consts, 1)
                pool.wait_ge(consts, n)

            link(nc.gpsimd.memset(ident[:, :], 0.0))
            constant(nc.gpsimd.affine_select(out=ident[:, :], in_=ident[:, :], compare_op=ALU.not_equal, fill=1.0,
                                             base=0, pattern=[[-1, P]], channel_multiplier=1), 1)
            link(nc.gpsimd.memset(mask[:, :], 0.0))
            constant(nc.gpsimd.affine_select(out=mask[:, :], in_=mask[:, :], compare_op=ALU.is_ge, fill=LOWEST,
                                             base=0, pattern=[[-1, P]], channel_multiplier=1), 2)
            constant(nc.gpsimd.memset(MX[:, :, :, :], LOWEST), 3)
            constant(nc.gpsimd.tensor_copy(ident_bf[:, :], ident[:, :]), 4)
            constant(nc.gpsimd.memset(VX[:, :, :, HD:2 * HD], 1.0), 5)
            constant(nc.gpsimd.memset(KS[ROWS:NROW, :, :].rearrange("p g t -> p (g t)").bitcast(F32), ONE_ONE), 6)
            pool.wait_ge(ab_in, 16 * (NC + 2))
            for c in range(NC):
                nc.gpsimd.tensor_tensor(b_raw[:, c, :, :], b_raw[:, c, :, :],
                                        coef[:, :].unsqueeze(2).broadcast_to([P, N_LORA, RANK]),
                                        ALU.mult).then_inc(b_scaled, 1)
            pool.wait_ge(bo_in, 32)
            pool.wait_ge(job_done, 2 * NC)
            for b in range(NT):
                nc.gpsimd.tensor_tensor(X[:, b, :], X[:, b, :], bo_bc[:, :], ALU.add).then_inc(xr_ready, 1)

            def split_wo(c):
                if c == 0:
                    pool.wait_ge(wo_in, 16)
                    pool.wait_ge(job_done, NJOB)
                link(nc.gpsimd.tensor_copy(WQ[:, 0, c, 0:D], wo_raw[:, c, :]))
                nc.gpsimd.tensor_tensor(WQ[:, 1, c, 0:D], wo_raw[:, c, :], WQ[:, 0, c, 0:D].bitcast(F32),
                                        ALU.subtract).then_inc(wo_split, 1)

            for cyc, (u, kb) in enumerate(CYCLES):
                d = kb - TB * half_of(u)
                if d >= 0:
                    for pair in range(2):
                        pool.wait_ge(probs, 2 * cyc + pair + 1)
                        blk = PB[:, cyc % NP_BUF, 2 * pair:2 * pair + 2, d * P:(d + 1) * P]
                        nc.gpsimd.affine_select(out=blk, in_=blk, compare_op=ALU.is_ge, fill=0.0, base=0,
                                                pattern=[[0, 2], [1, P]], channel_multiplier=-1)\
                            .then_inc(masked, 1)
                if half_of(u) == 1 and kb == 0 and u - G < NC:
                    split_wo(u - G)
            for b in range(NT):
                pool.wait_ge(x1_ready, b + 1)
                if b >= 2:
                    pool.wait_ge(y2_read, b - 1)
                nc.gpsimd.tensor_tensor(X1B[b % 2], X1[b % 3], bias_bc[:, :], ALU.add).then_inc(x1b_ready, 1)

        @block.scalar
        def _(act):
            for n, (kind, h, c) in enumerate(JOBS):
                if (kind, h, c) not in COPIED:
                    continue
                if kind == "WE":
                    if c == 0:
                        act.wait_ge(job_done, JOB[("Q", 1, NC - 1)] + 1)
                    act.wait_ge(job_done, n + 1)
                    nc.scalar.activation(WE[:, c, :], job_bank(n), ACT.Copy).then_inc(act_copied, 1)
                    continue
                act.wait_ge(job_done, n + 1)
                if kind == "xT":
                    nc.scalar.activation(xT[:, c, h * HT:(h + 1) * HT], job_bank(n), ACT.Copy)\
                        .then_inc(act_copied, 1)
                else:
                    m = PROJ.index((kind, h, c))
                    if m >= 2:
                        act.wait_ge(parts_out[m % 2], 16 * (m // 2))
                        act.wait_ge(parts_ready, m - 1)
                    nc.scalar.activation(parts[:, m % 2, 0, :], job_bank(n), ACT.Copy).then_inc(act_copied, 1)

            def turn_rows(u):
                act.wait_ge(nm_turned, u + 1)
                if u >= 2:
                    act.wait_ge(nm_out, 16 * (u - 1))
                nc.scalar.activation(NMR[0:NPART * REP, u % 2, :], PS[0:NPART * REP, MISC, :], ACT.Copy)\
                    .then_inc(nm_rows, 1)

            def evacuate(u):
                last = FIRST[u + 1] if u + 1 < NU else NCYC
                act.wait_ge(pv_done, last)
                if u >= G + NC:
                    act.wait_ge(wo_split, NC)
                nc.scalar.activation(RAW[:, u, :], PS[:, PV_BANK, :], ACT.Copy).then_inc(raw_out, 1)

            turn_rows(0)
            act.wait_ge(job_freed, NJOB)
            for cyc, (u, kb) in enumerate(CYCLES):
                d = max(0, kb - TB * half_of(u))
                for pair in range(2):
                    e = 2 * cyc + pair
                    act.wait_ge(scores, e + 1)
                    if cyc >= NP_BUF:
                        act.wait_ge(pv_done, cyc - NP_BUF + 1)
                    nc.scalar.activation(PB[:, cyc % NP_BUF, 2 * pair:2 * pair + 2, d * P:HT],
                                         PS[:, ST0 + 2 * pair:ST0 + 2 * pair + 2, 0:HT - d * P],
                                         ACT.Exp, scale=SCALE).then_inc(probs, 1)
                if kb == 0 and u:
                    evacuate(u - 1)
                for v in range(1, NU):
                    if rows_cycle(v) == cyc:
                        turn_rows(v)
            evacuate(NU - 1)

            def root(n):
                act.wait_ge(ln_var, n + 1)
                nc.scalar.activation(std[:, n % 4:n % 4 + 1], mv[:, n % 4, 1:2], ACT.Sqrt).then_inc(ln_std, 1)

            norm = 0
            for i in range(NT + 3):
                if 0 <= i - 1 < NT:
                    b = i - 1
                    act.wait_ge(t2_done, b + 1)
                    if b >= 2:
                        act.wait_ge(wo_done, b - 1)
                    nc.scalar.activation(CT[:, b % 2, 0, :, :], PS[:, 4, :].rearrange("p (c t) -> p c t", c=NC),
                                         ACT.Copy).then_inc(ct_hi, 1)
                if 0 <= i - 3 < NT:
                    root(norm)
                    norm += 1
                if 0 <= i - 1 < NT:
                    root(norm)
                    norm += 1
                if 0 <= i - 2 < NT:
                    b = i - 2
                    act.wait_ge(t3_done, b + 1)
                    if b >= 2:
                        act.wait_ge(ffn_done, b - 1)
                    nc.scalar.activation(X1T[:, b % 2, 0, :, :], PS[:, 6, :].rearrange("p (c t) -> p c t", c=NC),
                                         ACT.Copy).then_inc(x1_hi, 1)

        @block.vector
        def _(dve):
            step = [0]

            def link(ins):
                step[0] += 1
                ins.then_inc(dve_step, 1)
                dve.wait_ge(dve_step, step[0])

            def item_max(i):
                u, qb, j = item(i)
                k = i % 16
                par = u % 2
                done = chunks_before(i)
                if half_of(u):
                    dve.wait_ge(max_scores, done + 1)
                    nc.vector.tensor_reduce(MX[:, par, k, 0:1], PS[:, MAX0 + done % 2, :], AX, ALU.max)\
                        .then_inc(max_read, 1)
                    done += 1
                dve.wait_ge(max_scores, done + 1)
                bank = PS[:, MAX0 + done % 2, :]
                if qb:
                    nc.vector.tensor_reduce(MX[:, par, k, 1:2], bank[:, 0:qb * P], AX, ALU.max)
                nc.vector.tensor_tensor_reduce(out=scrap[:, i % 2, :], in0=bank[:, qb * P:(qb + 1) * P],
                                               in1=mask[:, :], scale=1.0, scalar=LOWEST, op0=ALU.add,
                                               op1=ALU.max, accum_out=MX[:, par, k, 2:3]).then_inc(max_read, 1)
                if k == 15:
                    finish_maxima(u, chunks_before(i + 1))

            def finish_maxima(u, chunks):
                par = u % 2

                def view(t):
                    return t.rearrange("p (q j) -> p q j", j=REP)
                dve.wait_ge(max_read, chunks)
                link(nc.vector.tensor_reduce(NM[:, par, :], MX[:, par, :, :], AX, ALU.max, negate=True))
                if u >= 2:
                    dve.wait_ge(nm_turned, u - 1)
                link(nc.vector.tensor_copy(NMP[:, par, :, 0, :], view(NM[:, par, :])))
                link(nc.vector.tensor_tensor(view(NM2[:, par, :]), view(NM[:, par, :]), NMP[:, par, :, 0, :],
                                             ALU.subtract))
                link(nc.vector.tensor_copy(NMP[:, par, :, 1, :], view(NM2[:, par, :])))
                nc.vector.tensor_tensor(NMP[:, par, :, 2, :], view(NM2[:, par, :]), NMP[:, par, :, 1, :],
                                        ALU.subtract).then_inc(nm_parts, 1)

            dve.wait_ge(wkv_in, 16)
            for c in range(NC):
                keys = wkv_v[:, c, 0, :, :]
                hi = WQ[:, 0, c, D:D + KD].rearrange("p (g d) -> p g d", d=HD)
                lo = WQ[:, 1, c, D:D + KD].rearrange("p (g d) -> p g d", d=HD)
                link(nc.vector.tensor_copy(hi, keys))
                nc.vector.tensor_tensor(lo, keys, hi.bitcast(F32), ALU.subtract).then_inc(wk_split, 1)
            copied = 0
            projected = 0
            issued = 0
            for n, (kind, h, c) in enumerate(JOBS):
                half = slice(h * HT, (h + 1) * HT)
                bank = job_bank(n)
                if kind in ("xT", "K", "Q", "WE"):
                    copied += 1
                    dve.wait_ge(act_copied, copied)
                if kind == "xT":
                    link(nc.vector.tensor_copy(XT[:, 0, c, half], xT[:, c, half]))
                    nc.vector.tensor_tensor(XT[:, 1, c, half], bank, XT[:, 0, c, half].bitcast(F32),
                                            ALU.subtract).then_inc(job_freed, 1)
                    if n == NC - 1:
                        dve.wait_ge(wq_in, 16)
                        for cc in range(NC):
                            link(nc.vector.tensor_copy(WQ[:, 0, cc, 0:D], wq_raw[:, cc, :]))
                            nc.vector.tensor_tensor(WQ[:, 1, cc, 0:D], wq_raw[:, cc, :],
                                                    WQ[:, 0, cc, 0:D].bitcast(F32), ALU.subtract)\
                                .then_inc(wq_split, 1)
                elif kind == "V":
                    dve.wait_ge(job_done, n + 1)
                    nc.vector.tensor_copy(VX[:, h * TB:(h + 1) * TB, :, 0:HD],
                                          bank.rearrange("p (b g d) -> p b g d", b=TB, d=HD))\
                        .then_inc(job_freed, 1)
                elif kind in "KQ":
                    s = projected % 2
                    nc.vector.tensor_tensor(rest[:, s, :], bank, parts[:, s, 0, :], ALU.subtract)\
                        .then_inc(job_freed, 1)
                    dve.wait_ge(job_freed, n + 1)
                    link(nc.vector.tensor_copy(parts[:, s, 1, :], rest[:, s, :]))
                    nc.vector.tensor_tensor(parts[:, s, 2, :], rest[:, s, :], parts[:, s, 1, :],
                                            ALU.subtract).then_inc(parts_ready, 1)
                    projected += 1
                elif kind == "bT":
                    dve.wait_ge(job_done, n + 1)
                    nc.vector.tensor_scalar(bT[:, :], bank, LORA_SCALE, None, ALU.mult)\
                        .then_inc(job_freed, 1)
                elif kind == "WE":
                    nc.vector.tensor_tensor(WEL[:, c, :], bank, WE[:, c, :].bitcast(F32), ALU.subtract)\
                        .then_inc(job_freed, 1)
                while issued < early_items(n):
                    if issued == 0:
                        dve.wait_ge(consts, 6)
                    item_max(issued)
                    issued += 1
            for i in range(issued, 16 * NU):
                item_max(i)

            norm = [0]

            def normalise(y, result, ready):
                n = norm[0]
                norm[0] += 1
                s = n % 4
                link(nc.vector.bn_stats(stats[:, s, :], y))
                link(nc.vector.bn_aggr(mv[:, s, :], stats[:, s, :]))
                nc.vector.tensor_scalar_add(mv[:, s, 1:2], mv[:, s, 1:2], EPS).then_inc(ln_var, 1)
                dve.wait_ge(ln_std, n + 1)
                link(nc.vector.reciprocal(rstd[:, s:s + 1], std[:, s:s + 1]))
                nc.vector.tensor_scalar(result, y, mv[:, s, 0:1], rstd[:, s:s + 1], ALU.subtract, ALU.mult)\
                    .then_inc(ready, 1)

            for i in range(NT + 3):
                if 0 <= i - 1 < NT:
                    b = i - 1
                    dve.wait_ge(ct_hi, b + 1)
                    nc.vector.tensor_tensor(CT[:, b % 2, 1, :, :], PS[:, 4, :].rearrange("p (c t) -> p c t", c=NC),
                                            CT[:, b % 2, 0, :, :].bitcast(F32), ALU.subtract).then_inc(ct_ready, 1)
                if i < NT:
                    b = i
                    dve.wait_ge(t1_done, b + 1)
                    both = PS[:, 2 * (b % 2):2 * (b % 2) + 2, :].rearrange("p a n -> p (a n)")\
                        .rearrange("p (h e) -> p h e", e=2 * HD)
                    if b >= 2:
                        dve.wait_ge(t2_done, b - 1)
                    link(nc.vector.reciprocal(rec[:, b % 2, :], both[:, :, HD]))
                    nc.vector.tensor_tensor(CTX[b % 2].rearrange("p (h d) -> p h d", d=HD), both[:, :, 0:HD],
                                            rec[:, b % 2, :].unsqueeze(2).broadcast_to([P, H, HD]), ALU.mult)\
                        .then_inc(ctx_ready, 1)
                if 0 <= i - 3 < NT:
                    b = i - 3
                    dve.wait_ge(ffn_done, b + 1)
                    dve.wait_ge(x1b_ready, b + 1)
                    nc.vector.tensor_tensor(Y2[b % 2], PS[:, 7, :], X1B[b % 2], ALU.add).then_inc(y2_read, 1)
                    dve.wait_ge(y2_read, b + 1)
                    if b >= 2:
                        dve.wait_ge(out_done[b % 2], 16 * (b // 2))
                    normalise(Y2[b % 2], OUT[b % 2], out_ready)
                if 0 <= i - 1 < NT:
                    b = i - 1
                    dve.wait_ge(wo_done, b + 1)
                    if b == 0:
                        dve.wait_ge(xr_ready, NT)
                    nc.vector.tensor_tensor(Y1[b % 2], PS[:, 5, :], X[:, b, :], ALU.add).then_inc(y1_read, 1)
                    dve.wait_ge(y1_read, b + 1)
                    if b >= 3:
                        dve.wait_ge(x1b_ready, b - 2)
                        dve.wait_ge(t3_done, b - 2)
                    normalise(Y1[b % 2], X1[b % 3], x1_ready)
                if 0 <= i - 2 < NT:
                    b = i - 2
                    dve.wait_ge(x1_hi, b + 1)
                    nc.vector.tensor_tensor(X1T[:, b % 2, 1, :, :], PS[:, 6, :].rearrange("p (c t) -> p c t", c=NC),
                                            X1T[:, b % 2, 0, :, :].bitcast(F32), ALU.subtract).then_inc(x1t_ready, 1)

        @block.tensor
        def _(pe):
            def item_scores(i):
                u, qb, j = item(i)
                h, g = divmod(u, G)
                if i % 16 == 0:
                    pe.wait_ge(qs_in[u % SLOTS], 96 * (u // SLOTS + 1))
                    if u == 0:
                        pe.wait_ge(ks_in[0], 96)
                    if u == G:
                        pe.wait_ge(ks_in[1], 96)
                n = chunks_before(i)
                for k0 in range(0, h * HT + 1, HT):
                    width = HT if k0 < h * HT else (qb + 1) * P
                    if n >= 2:
                        pe.wait_ge(max_read, n - 1)
                    nc.tensor.matmul(PS[:, MAX0 + n % 2, 0:width],
                                     QS[0:ROWS, u % SLOTS, j, qb * P:(qb + 1) * P],
                                     KS[0:ROWS, g, k0:k0 + width], start=True, stop=True)\
                        .then_inc(max_scores, 1)
                    n += 1

            def turn_maxima(u):
                pe.wait_ge(nm_parts, u + 1)
                if u:
                    pe.wait_ge(nm_rows, u)
                for qb in range(TB):
                    last = nc.tensor.matmul(PS[0:NPART * REP, MISC, qb * P:(qb + 1) * P],
                                            NMP[:, u % 2, qb, :, :].rearrange("p a j -> p (a j)"),
                                            ident_bf[:, :], start=True, stop=True)
                last.then_inc(nm_turned, 1)

            def three(bank, lhs, rhs):
                terms = [(0, 0), (0, 1), (1, 0)]
                for c in range(NC):
                    for k, (a, b) in enumerate(terms):
                        last = nc.tensor.matmul(bank, lhs(a, c), rhs(b, c), start=(c == 0 and k == 0),
                                                stop=(c == NC - 1 and k == 2))
                return last

            issued = 0
            pe.wait_ge(consts, 1)
            for n, (kind, h, c) in enumerate(JOBS):
                bank = job_bank(n)
                half = slice(h * HT, (h + 1) * HT)
                if n >= RING:
                    pe.wait_ge(job_freed, n - RING + 1)
                if kind == "xT":
                    if c == 0:
                        pe.wait_ge(x_in[h], 16)
                    for b in range(TB):
                        last = nc.tensor.transpose(bank[:, b * P:(b + 1) * P],
                                                   X[:, h * TB + b, c * P:(c + 1) * P], ident[:, :])
                elif kind == "V":
                    pe.wait_ge(wkv_in, 16)
                    pe.wait_ge(act_copied, NC * (h + 1))
                    for b in range(TB):
                        for cc in range(NC):
                            t0 = h * HT + b * P
                            last = nc.tensor.matmul(bank[:, b * P:(b + 1) * P], xT[:, cc, t0:t0 + P],
                                                    wkv_v[:, cc, 1, :, :], start=(cc == 0), stop=(cc == NC - 1))
                elif kind == "K":
                    pe.wait_ge(wk_split, NC)
                    pe.wait_ge(job_freed, NC * (h + 1))
                    last = three(bank, lambda a, cc: WQ[:, a, cc, D:D + KD], lambda a, cc: XT[:, a, cc, half])
                elif kind == "Q":
                    pe.wait_ge(wq_split, NC)
                    last = three(bank, lambda a, cc: WQ[:, a, cc, c * P:(c + 1) * P],
                                 lambda a, cc: XT[:, a, cc, half])
                elif kind == "bT":
                    pe.wait_ge(b_scaled, NC)
                    for cc in range(NC):
                        last = nc.tensor.transpose(bank[:, cc * P:(cc + 1) * P],
                                                   b_raw[:, cc, :, :].rearrange("p n r -> p (n r)"), ident[:, :])
                elif kind == "WE":
                    pe.wait_ge(w_in, 16)
                    pe.wait_ge(job_freed, JOB[("bT", 0, 0)] + 1)
                    nc.tensor.matmul(bank, a_raw[:, c * P:(c + 1) * P], bT[:, :], start=True, stop=False)
                    for o in range(NC):
                        last = nc.tensor.matmul(bank[:, o * P:(o + 1) * P], w_raw[:, o, c * P:(c + 1) * P],
                                                ident[:, :], start=False, stop=(o == NC - 1))
                last.then_inc(job_done, 1)
                while issued < early_items(n):
                    if issued == 0:
                        pe.wait_ge(consts, 6)
                    item_scores(issued)
                    issued += 1
            while issued < items_due(0):
                item_scores(issued)
                issued += 1
            pe.wait_ge(job_freed, NJOB)
            turn_maxima(0)

            def accumulate(cyc):
                u, kb = CYCLES[cyc]
                g = u % G
                d = kb - TB * half_of(u)
                if d >= 0:
                    diag = sum(1 for v, k in CYCLES[:cyc + 1] if k >= TB * half_of(v))
                    pe.wait_ge(masked, 2 * diag)
                pe.wait_ge(probs, 2 * cyc + 2)
                d = max(d, 0)
                if kb == 0 and u:
                    pe.wait_ge(raw_out, u)
                n_kb = TB * (1 + half_of(u))
                for j in range(REP):
                    last = nc.tensor.matmul(PS[32 * j:32 * j + 32, PV_BANK, d * P:HT], VX[:, kb, g, :],
                                            PB[:, cyc % NP_BUF, j, d * P:HT], start=(kb == 0),
                                            stop=(kb == n_kb - 1))
                last.then_inc(pv_done, 1)

            for cyc, (u, kb) in enumerate(CYCLES):
                d = max(0, kb - TB * half_of(u))
                if kb == 0:
                    pe.wait_ge(nm_in, 16 * (u + 1))
                todo = items_due(cyc + 1) - issued
                for pair in range(2):
                    e = 2 * cyc + pair
                    if e >= 2:
                        pe.wait_ge(probs, e - 1)
                    for j in range(2 * pair, 2 * pair + 2):
                        last = nc.tensor.matmul(PS[:, ST0 + j, 0:HT - d * P],
                                                KS[0:NROW, u % G, kb * P:(kb + 1) * P],
                                                QS[0:NROW, u % SLOTS, j, d * P:HT], start=True, stop=True)
                    last.then_inc(scores, 1)
                    for _ in range(todo // 2 if pair == 0 else todo - todo // 2):
                        item_scores(issued)
                        issued += 1
                for v in range(1, NU):
                    if rows_cycle(v) == cyc:
                        turn_maxima(v)
                if cyc:
                    accumulate(cyc - 1)
            accumulate(NCYC - 1)

            pe.wait_ge(max_read, chunks_before(16 * NU))
            pe.wait_ge(wo_split, NC)
            pe.wait_ge(nm_rows, NU)
            pe.wait_ge(probs, 2 * NCYC)
            pe.wait_ge(raw_out, NU)
            for i in range(NT + 3):
                if 0 <= i - 1 < NT:
                    b = i - 1
                    pe.wait_ge(ctx_ready, b + 1)
                    if b:
                        pe.wait_ge(ct_ready, b)
                    for c in range(NC):
                        last = nc.tensor.transpose(PS[:, 4, c * P:(c + 1) * P], CTX[b % 2][:, c * P:(c + 1) * P],
                                                   ident[:, :])
                    last.then_inc(t2_done, 1)
                if i < NT:
                    b = i
                    h, qb = divmod(b, TB)
                    if b >= 2:
                        pe.wait_ge(ctx_ready, b - 1)
                    for g in range(G):
                        last = nc.tensor.transpose(
                            PS[:, 2 * (b % 2) + g // 4, (g % 4) * P:(g % 4 + 1) * P],
                            RAW[:, h * G + g, qb * P:(qb + 1) * P], ident[:, :])
                    last.then_inc(t1_done, 1)
                if 0 <= i - 3 < NT:
                    b = i - 3
                    pe.wait_ge(x1t_ready, b + 1)
                    if b:
                        pe.wait_ge(y2_read, b)
                    three(PS[:, 7, :], lambda a, c: X1T[:, b % 2, a, c, :],
                          lambda a, c: (WEL if a else WE)[:, c, :]).then_inc(ffn_done, 1)
                if 0 <= i - 1 < NT:
                    b = i - 1
                    pe.wait_ge(ct_ready, b + 1)
                    if b:
                        pe.wait_ge(y1_read, b)
                    three(PS[:, 5, :], lambda a, c: CT[:, b % 2, a, c, :], lambda a, c: WQ[:, a, c, 0:D])\
                        .then_inc(wo_done, 1)
                if 0 <= i - 2 < NT:
                    b = i - 2
                    pe.wait_ge(x1_ready, b + 1)
                    if b:
                        pe.wait_ge(x1t_ready, b)
                    for c in range(NC):
                        last = nc.tensor.transpose(PS[:, 6, c * P:(c + 1) * P], X1[b % 3][:, c * P:(c + 1) * P],
                                                   ident[:, :])
                    last.then_inc(t3_done, 1)


_INS = ["L0_attn_x", "L0_attn_Wq", "L0_attn_Wkv", "L0_attn_Wo", "L0_attn_bo", "L0_ffn_lora_A", "L0_ffn_lora_B",
        "L0_ffn_W", "L0_ffn_bias", "L0_ffn_lora_weights"]
_OUTS = [((1, 1024, 512), "float32")]


def kernel(**inputs):
    import numpy as _np
    import concourse.bacc as _bacc
    from concourse import mybir as _mybir
    from concourse.bass_utils import run_bass_kernel_spmd as _run

    nc = _bacc.Bacc("TRN2", target_bir_lowering=False, num_devices=1)
    arrays, args = {}, []
    for name in _INS:
        a = _np.ascontiguousarray(inputs[name])
        arrays[f"in_{name}_dram"] = a
        args.append(nc.dram_tensor(f"in_{name}_dram", a.shape, _mybir.dt.from_np(a.dtype), kind="ExternalInput").ap())
    for i, (shape, dtype) in enumerate(_OUTS):
        dt = _mybir.dt.from_np(_np.dtype(dtype))
        args.append(nc.dram_tensor(f"out_{i}_dram", shape, dt, kind="ExternalOutput").ap())
    postln_kernel(nc, *args)
    r = _run(nc, [arrays], core_ids=[0])
    got = tuple(r.results[0][f"out_{i}_dram"] for i in range(len(_OUTS)))
    return got[0]
```

```python
import numpy as np
import concourse.bass as bass
from concourse import mybir
from contextlib import ExitStack

F32 = mybir.dt.float32
F32R = mybir.dt.float32r
BF16 = mybir.dt.bfloat16
ACT = mybir.ActivationFunctionType
ALU = mybir.AluOpType
AX = mybir.AxisListType.X

P = 128
LOWEST = -3.0e38
EPS = 1e-5
ONE_ONE = float(np.array([0x3F803F80], np.uint32).view(np.float32)[0])
ALPHA = 32


def postln_kernel(nc, x, wq, wkv, wo, bo, lora_a, lora_b, w, bias, lora_w, out):
    _, T, D = x.shape
    N_LORA, RANK, _ = lora_a.shape
    HD = 16
    H = D // HD
    G = wkv.shape[1] // (2 * HD)
    REP = H // G
    NC = D // P
    NT = T // P
    HT = T // 2
    TB = HT // P
    KD = G * HD
    HC = P // HD
    SCALE = 1.0 / HD ** 0.5
    LORA_SCALE = ALPHA / RANK
    assert KD == P and N_LORA * RANK == P and D == HT == 512 and REP == 4 and NC == TB == 4

    NPART = 3
    ROWS = 6 * HD
    NROW = ROWS + NPART

    NU = 2 * G
    CYCLES = [(u, kb) for u in range(NU) for kb in range(TB * (1 + u // G))]
    FIRST = [CYCLES.index((u, 0)) for u in range(NU)]
    NCYC = len(CYCLES)
    ITEMS = TB * REP
    LEAD = 4
    SLOTS = 5
    NP_BUF = 3
    HEAVY = 2.3

    def half_of(u):
        return u // G

    def items_due(c):
        level = FIRST[G] - LEAD
        if c >= level:
            if c + LEAD >= NCYC:
                return ITEMS * NU
            v, o = CYCLES[c + LEAD]
            return min(ITEMS * NU, ITEMS * (v + 1) + ITEMS * o // (2 * TB))
        light = ITEMS * (G - 2)
        work = (light + ITEMS * HEAVY) * c / level
        return 2 * ITEMS + int(min(work, light) + max(0.0, work - light) / HEAVY)

    def chunks_before(i):
        return i if i <= ITEMS * G else 2 * i - ITEMS * G

    def item(i):
        u, k = divmod(i, ITEMS)
        return u, k // REP, k % REP

    def chunks_of_cycle(c):
        lot = [(i, k) for i in range(items_due(c), items_due(c + 1)) for k in range(1 + half_of(i // ITEMS))]
        return [lot[len(lot) * q // 4:len(lot) * (q + 1) // 4] for q in range(4)]

    def rows_cycle(u):
        return FIRST[u] - LEAD + 1 if u else -1

    ROWS_AT = {rows_cycle(u): u for u in range(1, NU)}

    JOBS = [("xT", 0, c) for c in range(NC)]
    JOBS += [("K", 0, 0), ("Q", 0, 0), ("V", 0, 0), ("Q", 0, 1), ("Q", 0, 2)]
    JOBS += [("xT", 1, c) for c in range(NC)]
    JOBS += [("Q", 0, 3), ("V", 1, 0), ("K", 1, 0)]
    NJOB_A = len(JOBS)
    LATER = [("Q", 1, c) for c in range(NC)] + [("bT", 0, 0)] + [("WE", 0, c) for c in range(NC)]
    JOBS += LATER
    JOB = {job: n for n, job in enumerate(JOBS)}
    RING = 4
    PROJ = [j for j in JOBS if j[0] in "KQ"]
    PROJ_A = sum(1 for j in JOBS[:NJOB_A] if j[0] in "KQ")

    STEPS = [(kind, b, 0) for b in range(TB) for kind in ("T1a", "T1b", "T2", "WO", "T3", "FF")]
    FILL = {2 * n: job for n, job in enumerate(LATER)}
    FILL.update({FIRST[G] + 2 * (n + 1): job for n, job in enumerate(STEPS)})
    assert max(FILL) < NCYC and not set(FILL) & set(ROWS_AT)

    B0 = TB
    TAIL = [("T1", 0), ("T1", 1), ("T2", 0), ("T2", 1), ("T1", 2), ("WO", 0), ("T1", 3), ("T2", 2), ("WO", 1),
            ("T2", 3), ("WO", 2), ("T3", 0), ("WO", 3), ("T3", 1), ("FF", 0), ("T3", 2), ("FF", 1), ("T3", 3),
            ("FF", 2), ("FF", 3)]
    TAIL_DVE = [("T1", 0), ("T1", 1), ("T2", 0), ("T2", 1), ("T1", 2), ("WO", 0), ("T1", 3), ("N1", 0), ("T2", 2),
                ("WO", 1), ("T2", 3), ("N1", 1), ("WO", 2), ("T3", 0), ("N1", 2), ("WO", 3), ("T3", 1), ("N1", 3),
                ("FF", 0), ("T3", 2), ("N2", 0), ("FF", 1), ("T3", 3), ("N2", 1), ("FF", 2), ("N2", 2), ("FF", 3),
                ("N2", 3)]
    TAIL_POOL = [("root", 0), ("bias", 0), ("root", 1), ("bias", 1), ("root", 2), ("root", 3), ("root", 0),
                 ("bias", 2), ("root", 1), ("bias", 3), ("root", 2), ("root", 3)]

    def tail_bank(kind, i):
        return {"T1": 2 * (i % 2), "T2": 4 + i % 2, "T3": 4 + i % 2, "WO": 6 + i % 2, "FF": i}[kind]

    def early_items(n):
        count = 0
        for kind, _, _ in JOBS[JOB[("Q", 0, 2)] + 1:n + 1]:
            count += 2 if kind == "xT" else 8
        return min(items_due(0), count)

    ctx = ExitStack()
    with ctx:
        def sb(name, shape, dt=F32):
            return ctx.enter_context(nc.sbuf_tensor(name, shape, dt))

        def sem(name):
            return ctx.enter_context(nc.semaphore(name))

        X = sb("X", [P, NT, D])
        RAW = sb("RAW", [P, NU, HT])
        xT = RAW[:, 0:G, :].rearrange("p a b -> p (a b)").rearrange("p (c t) -> p c t", c=NC)
        wq_raw = RAW[:, G:G + 4, :]
        w_raw = RAW[:, G:G + 4, :]
        wo_raw = RAW[:, G + 4:G + 8, :]
        XT = sb("XT", [P, 2, NC, T], F32R)
        WE = XT[:, 0, :, 0:D]
        WEL = XT[:, 1, :, 0:D]
        CT = XT[:, :, :, D:D + 2 * P].rearrange("p a c (b t) -> p b a c t", b=2)
        X1T = XT[:, :, :, D + 2 * P:D + 4 * P].rearrange("p a c (b t) -> p b a c t", b=2)
        WQ = sb("WQ", [P, 2, NC, D + KD], F32R)
        QS = sb("QS", [P, SLOTS, REP, HT], BF16)
        KS = sb("KS", [P, G, T], BF16)
        VX = sb("VX", [P, NT, G, 2 * HD])
        PB = sb("PB", [P, NP_BUF, REP, HT])
        parts = sb("parts", [P, 2, NPART, HT], BF16)
        bias_bc = sb("bias_bc", [P, D])
        ident = sb("ident", [P, P])
        ident_bf = sb("ident_bf", [P, P], BF16)
        mask = sb("mask", [P, P])
        scrap = sb("scrap", [P, 4, P])
        coef = sb("coef", [P, N_LORA])
        MX = sb("MX", [P, 2, ITEMS, 3])
        NM = sb("NM", [P, 2, ITEMS])
        NM2 = sb("NM2", [P, 2, ITEMS])
        NMP = sb("NMP", [P, 2, TB, NPART, REP], BF16)
        NMR = sb("NMR", [P, 2, HT], BF16)
        stats = sb("stats", [P, 4, 6])
        mv = sb("mv", [P, 4, 2])
        minus_half = sb("minus_half", [P, 1])
        rstd = sb("rstd", [P, 4])
        rec = sb("rec", [P, 4, H // 2])

        TC = sb("TC", [P, 9, D])
        CTX = [TC[:, 0, :], TC[:, 1, :]]
        X1 = [TC[:, 2, :], TC[:, 3, :]]
        X1B = [TC[:, 4, :], TC[:, 5, :]]
        OUT = [TC[:, 6, :], TC[:, 7, :]]
        Y = TC[:, 8, :]
        a_raw, bT = TC[:, 0, :], TC[:, 8, :]
        b_raw = TC[:, 1, :].rearrange("p (c n r) -> p c n r", c=NC, n=N_LORA)
        wkv_raw = TC[:, 2:4, :].rearrange("p a n -> p (a n)").rearrange("p (c n) -> p c n", c=NC)
        wkv_v = wkv_raw.rearrange("p c (g two d) -> p c two g d", two=2, d=HD)
        bo_bc = TC[:, 4, :]
        rest = TC[:, 6:8, :]

        PS = ctx.enter_context(nc.psum_tensor("PS", [P, 8, 512], F32))
        MAX_BANKS, ST_BANKS = 3, 3
        PV_BANK, MISC = 6, 7

        scr_q = nc.dram_tensor("scr_q", (2, NC, NPART, P, HT), BF16).ap()
        scr_k = nc.dram_tensor("scr_k", (2, NPART, KD, HT), BF16).ap()
        scr_m = nc.dram_tensor("scr_m", (NU, NPART * REP, HT), BF16).ap()

        x_in = [sem(f"x_in{h}") for h in range(2)]
        wkv_in, wq_in, ab_in, w_in, wo_in, bo_in = (sem(n) for n in (
            "wkv_in", "wq_in", "ab_in", "w_in", "wo_in", "bo_in"))
        consts = sem("consts")
        job_done = sem("job_done")
        job_freed = sem("job_freed")
        xt32 = sem("xt32")
        act_copied = sem("act_copied")
        wk_split = sem("wk_split")
        wq_high, wq_split = sem("wq_high"), sem("wq_split")
        b_scaled, wo_split = sem("b_scaled"), sem("wo_split")
        rest_split = sem("rest_split")
        parts_ready = sem("parts_ready")
        parts_out = [sem(f"parts_out{b}") for b in range(2)]
        ks_in = [sem(f"ks_in{h}") for h in range(2)]
        qs_in = [sem(f"qs_in{s}") for s in range(SLOTS)]
        max_scores = sem("max_scores")
        max_read = sem("max_read")
        nm_parts = sem("nm_parts")
        nm_turned = sem("nm_turned")
        nm_rows = sem("nm_rows")
        nm_out = sem("nm_out")
        nm_in = sem("nm_in")
        scores = sem("scores")
        probs = sem("probs")
        masked = sem("masked")
        pv_done = sem("pv_done")
        raw_out = sem("raw_out")
        xr_ready = sem("xr_ready")
        dve_step, pool_step = sem("dve_step"), sem("pool_step")
        t1_done, t2_done, wo_done, t3_done, ffn_done = (sem(n) for n in (
            "t1_done", "t2_done", "wo_done", "t3_done", "ffn_done"))
        ctx_ready, ct_hi, ct_ready = sem("ctx_ready"), sem("ct_hi"), sem("ct_ready")
        ln_var, ln_root = sem("ln_var"), sem("ln_root")
        y1_read, x1_ready, x1_hi, x1t_ready = (sem(n) for n in ("y1_read", "x1_ready", "x1_hi", "x1t_ready"))
        x1b_ready, y2_read, out_ready = sem("x1b_ready"), sem("y2_read"), sem("out_ready")
        out_done = [sem(f"out_done{b}") for b in range(2)]

        def job_bank(n):
            return PS[:, 3 + n % RING if n < NJOB_A else MISC, :]

        def freed(job):
            kind, b, _ = job
            if kind == "rows":
                return nm_rows, b + 1
            if kind in ("T1a", "T1b"):
                return ctx_ready, 2 * b + (2 if kind == "T1b" else 1)
            if kind in ("T2", "WO", "T3", "FF"):
                return {"T2": ct_ready, "WO": y1_read, "T3": x1t_ready, "FF": y2_read}[kind], b + 1
            return job_freed, JOB[job] + 1

        MISC_ORDER = [("rows", 0, 0)] + [FILL[c] if c in FILL else ("rows", ROWS_AT[c], 0)
                                         for c in range(NCYC) if c in FILL or c in ROWS_AT]

        def blocks(bank):
            return bank.rearrange("p (c t) -> p c t", c=NC)

        x_v = x.rearrange("a (h b p) d -> (a h) p b d", h=2, p=P)
        out_v = out.rearrange("a (b p) d -> (a b) p d", p=P)

        block = ctx.enter_context(nc.Block())

        @block.sync
        def _(sp):
            sp.dma_start(X[:, 0:TB, :], x_v[0]).then_inc(x_in[0], 16)
            sp.dma_start(wkv_raw, wkv.rearrange("(c p) n -> p c n", p=P)).then_inc(wkv_in, 16)
            sp.dma_start(wq_raw, wq.rearrange("(c p) n -> p c n", p=P)).then_inc(wq_in, 16)
            sp.dma_start(X[:, TB:NT, :], x_v[1]).then_inc(x_in[1], 16)
            sp.dma_start(bo_bc, bo.partition_broadcast(P)).then_inc(bo_in, 16)
            sp.dma_start(bias_bc[:, :], bias.partition_broadcast(P)).then_inc(bo_in, 16)

            def parts_to_dram(n):
                kind, h, c = PROJ[n]
                sp.wait_ge(parts_ready, n + 1)
                dst = scr_k[h] if kind == "K" else scr_q[h, c]
                sp.dma_start(dst.rearrange("a p t -> p a t"), parts[:, n % 2, :, :])\
                    .then_inc(parts_out[n % 2], 16)

            def parts_landed(n):
                sp.wait_ge(parts_out[n % 2], 16 * (n // 2 + 1))

            def load_keys(h):
                parts_landed(PROJ.index(("K", h, 0)))
                row = 0
                for a, copies in enumerate((3, 2, 1)):
                    for _ in range(copies):
                        sp.dma_start(KS[row:row + HD, :, h * HT:(h + 1) * HT],
                                     scr_k[h, a].rearrange("(d g) t -> d g t", g=G)).then_inc(ks_in[h], 16)
                        row += HD

            def load_queries(u):
                h, g = divmod(u, G)
                slot = u % SLOTS
                c, j0 = divmod(g * REP, HC)
                if u >= SLOTS:
                    sp.wait_ge(scores, REP * FIRST[u - SLOTS + 1])
                parts_landed(PROJ.index(("Q", h, c)))
                row = 0
                for run in (3, 2, 1):
                    sp.dma_start(QS[row:row + run * HD, slot, :, :],
                                 scr_q[h, c, 0:run].rearrange("a (d j) t -> (a d) j t", j=HC)[:, j0:j0 + REP, :])\
                        .then_inc(qs_in[slot], 16)
                    row += run * HD

            def move_maxima(u):
                sp.wait_ge(nm_rows, u + 1)
                sp.dma_start(scr_m[u], NMR[0:NPART * REP, u % 2, :]).then_inc(nm_out, 16)
                sp.wait_ge(nm_out, 16 * (u + 1))
                sp.dma_start(QS[ROWS:NROW, u % SLOTS, :, :],
                             scr_m[u].rearrange("(a j) t -> a j t", a=NPART)).then_inc(nm_in, 16)
                sp.wait_ge(nm_in, 16 * (u + 1))

            def store(b):
                sp.wait_ge(out_ready, b + 1)
                sp.dma_start(out_v[b], OUT[b % 2]).then_inc(out_done[b % 2], 16)

            for n in range(PROJ_A):
                if n == PROJ_A - 1:
                    move_maxima(0)
                parts_to_dram(n)
                if n == 1:
                    load_keys(0)
                    load_queries(0)
                    load_queries(1)
                if n == 2:
                    sp.dma_start(wo_raw, wo.rearrange("(c p) n -> p c n", p=P)).then_inc(wo_in, 16)
                    sp.wait_ge(wq_split, NC)
                    sp.dma_start(w_raw, w.rearrange("(c p) n -> p c n", p=P)).then_inc(w_in, 16)
                    sp.dma_start(a_raw, lora_a.rearrange("n r d -> (n r) d")).then_inc(ab_in, 16)
                    for c in range(NC):
                        sp.dma_start(b_raw[:, c, :, :], lora_b[:, c * P:(c + 1) * P, :]
                                     .rearrange("n p r -> p n r")).then_inc(ab_in, 16)
                    sp.dma_start(coef[:, :], lora_w.partition_broadcast(P)).then_inc(ab_in, 16)
                if n == 3:
                    load_queries(2)
                    load_queries(3)
                if n == 4:
                    load_queries(4)
            load_keys(1)
            for cyc, (u, kb) in enumerate(CYCLES):
                if kb == 0 and 1 <= u and u + SLOTS - 1 < NU:
                    load_queries(u + SLOTS - 1)
                if FILL.get(cyc) in PROJ:
                    parts_to_dram(PROJ.index(FILL[cyc]))
                if cyc in ROWS_AT:
                    move_maxima(ROWS_AT[cyc])
                if cyc - 1 in FILL and FILL[cyc - 1][0] == "FF":
                    store(FILL[cyc - 1][1])
            for b in range(TB, NT):
                store(b)
            for s in range(2):
                sp.wait_ge(out_done[s], 16 * (NT // 2))

        @block.gpsimd
        def _(pool):
            step = [0]

            def link(ins):
                step[0] += 1
                ins.then_inc(pool_step, 1)
                pool.wait_ge(pool_step, step[0])

            def constant(ins, n):
                ins.then_inc(consts, 1)
                pool.wait_ge(consts, n)

            def low_part(n):
                pool.wait_ge(rest_split, n + 1)
                s = n % 2
                nc.gpsimd.tensor_tensor(parts[:, s, 2, :], rest[:, s, :], parts[:, s, 1, :], ALU.subtract)\
                    .then_inc(parts_ready, 1)

            link(nc.gpsimd.memset(ident[:, :], 0.0))
            constant(nc.gpsimd.affine_select(out=ident[:, :], in_=ident[:, :], compare_op=ALU.not_equal, fill=1.0,
                                             base=0, pattern=[[-1, P]], channel_multiplier=1), 1)
            link(nc.gpsimd.memset(mask[:, :], 0.0))
            constant(nc.gpsimd.affine_select(out=mask[:, :], in_=mask[:, :], compare_op=ALU.is_ge, fill=LOWEST,
                                             base=0, pattern=[[-1, P]], channel_multiplier=1), 2)
            constant(nc.gpsimd.memset(MX[:, :, :, :], LOWEST), 3)
            constant(nc.gpsimd.tensor_copy(ident_bf[:, :], ident[:, :]), 4)
            link(nc.gpsimd.memset(minus_half[:, :], -0.5))
            for c in range(NC):
                pool.wait_ge(wq_high, c + 1)
                nc.gpsimd.tensor_tensor(WQ[:, 1, c, 0:D].rearrange("p (k d j) -> p k d j", d=HD, j=HC),
                                        wq_raw[:, c, :].rearrange("p (k j d) -> p k d j", d=HD, j=HC),
                                        WQ[:, 0, c, 0:D].bitcast(F32).rearrange("p (k d j) -> p k d j", d=HD, j=HC),
                                        ALU.subtract).then_inc(wq_split, 1)
            low_part(0)
            low_part(1)
            constant(nc.gpsimd.memset(VX[:, :, :, HD:2 * HD], 1.0), 5)
            constant(nc.gpsimd.memset(KS[ROWS:NROW, :, :].rearrange("p g t -> p (g t)").bitcast(F32), ONE_ONE), 6)
            for n in range(2, PROJ_A):
                low_part(n)
            pool.wait_ge(ab_in, 16 * (NC + 2))
            for c in range(NC):
                nc.gpsimd.tensor_tensor(b_raw[:, c, :, :], b_raw[:, c, :, :],
                                        coef[:, :].unsqueeze(2).broadcast_to([P, N_LORA, RANK]),
                                        ALU.mult).then_inc(b_scaled, 1)
            pool.wait_ge(bo_in, 32)

            def residual_input(b):
                pool.wait_ge(job_done, JOB[("xT", 1, NC - 1)] + 1)
                nc.gpsimd.tensor_tensor(X[:, b, :], X[:, b, :], bo_bc, ALU.add).then_inc(xr_ready, 1)

            def split_wo(c):
                pool.wait_ge(wo_in, 16)
                pool.wait_ge(job_done, JOB[("Q", 1, NC - 1)] + 1)
                link(nc.gpsimd.tensor_copy(WQ[:, 0, c, 0:D], wo_raw[:, c, :]))
                nc.gpsimd.tensor_tensor(WQ[:, 1, c, 0:D], wo_raw[:, c, :], WQ[:, 0, c, 0:D].bitcast(F32),
                                        ALU.subtract).then_inc(wo_split, 1)

            roots = [0]

            def root():
                n = roots[0]
                roots[0] += 1
                pool.wait_ge(ln_var, n + 1)
                nc.gpsimd.tensor_tensor(rstd[:, n % 4:n % 4 + 1], mv[:, n % 4, 1:2], minus_half[:, 0:1], ALU.pow)\
                    .then_inc(ln_root, 1)

            def add_bias(b):
                pool.wait_ge(x1_ready, b + 1)
                if b >= 2:
                    pool.wait_ge(y2_read, b - 1)
                nc.gpsimd.tensor_tensor(X1B[b % 2], X1[b % 2], bias_bc[:, :], ALU.add).then_inc(x1b_ready, 1)

            for cyc, (u, kb) in enumerate(CYCLES):
                d = kb - TB * half_of(u)
                if d >= 0:
                    for pair in range(2):
                        pool.wait_ge(probs, REP * cyc + 2 * pair + 2)
                        blk = PB[:, cyc % NP_BUF, 2 * pair:2 * pair + 2, d * P:(d + 1) * P]
                        nc.gpsimd.affine_select(out=blk, in_=blk, compare_op=ALU.is_ge, fill=0.0, base=0,
                                                pattern=[[0, 2], [1, P]], channel_multiplier=-1)\
                            .then_inc(masked, 1)
                if FILL.get(cyc) in PROJ:
                    low_part(PROJ.index(FILL[cyc]))
                if u < G and kb == 1:
                    residual_input(u)
                if G - NC <= u < G and kb == 3:
                    split_wo(u - (G - NC))
                if cyc - 1 in FILL and FILL[cyc - 1][0] == "WO":
                    add_bias(FILL[cyc - 1][1])
                if cyc in FILL and FILL[cyc][0] in ("WO", "FF"):
                    root()
            for kind, i in TAIL_POOL:
                if kind == "root":
                    root()
                else:
                    add_bias(B0 + i)

        @block.scalar
        def _(act):
            def act_job(n):
                kind, h, c = JOBS[n]
                if kind in ("V", "bT"):
                    return
                act.wait_ge(job_done, n + 1)
                if kind == "xT":
                    half = slice(h * HT, (h + 1) * HT)
                    nc.scalar.activation(xT[:, c, half], job_bank(n), ACT.Copy).then_inc(xt32, 1)
                    nc.scalar.activation(XT[:, 0, c, half], job_bank(n), ACT.Copy).then_inc(act_copied, 1)
                elif kind == "WE":
                    nc.scalar.activation(WE[:, c, :], job_bank(n), ACT.Copy).then_inc(act_copied, 1)
                else:
                    m = PROJ.index((kind, h, c))
                    if m >= 2:
                        act.wait_ge(parts_out[m % 2], 16 * (m // 2))
                    nc.scalar.activation(parts[:, m % 2, 0, :], job_bank(n), ACT.Copy).then_inc(act_copied, 1)

            def turn_rows(u):
                act.wait_ge(nm_turned, u + 1)
                if u >= 2:
                    act.wait_ge(nm_out, 16 * (u - 1))
                nc.scalar.activation(NMR[0:NPART * REP, u % 2, :], PS[0:NPART * REP, MISC, :], ACT.Copy)\
                    .then_inc(nm_rows, 1)

            def evacuate(u):
                last = FIRST[u + 1] if u + 1 < NU else NCYC
                act.wait_ge(pv_done, last)
                if u >= G + 4:
                    act.wait_ge(wo_split, NC)
                nc.scalar.activation(RAW[:, u, :], PS[:, PV_BANK, :], ACT.Copy).then_inc(raw_out, 1)

            def context_high(b, bank):
                act.wait_ge(t2_done, b + 1)
                if b >= 2:
                    act.wait_ge(wo_done, b - 1)
                nc.scalar.activation(CT[:, b % 2, 0, :, :], blocks(PS[:, bank, :]), ACT.Copy).then_inc(ct_hi, 1)

            def x1_high(b, bank):
                act.wait_ge(t3_done, b + 1)
                if b >= 2:
                    act.wait_ge(ffn_done, b - 1)
                nc.scalar.activation(X1T[:, b % 2, 0, :, :], blocks(PS[:, bank, :]), ACT.Copy).then_inc(x1_hi, 1)

            for n in range(NJOB_A):
                if n == NJOB_A - 1:
                    turn_rows(0)
                act_job(n)
                if n == NC - 1:
                    act.wait_ge(wq_in, 16)
                    for c in range(NC):
                        nc.scalar.activation(WQ[:, 0, c, 0:D].rearrange("p (k d j) -> p k d j", d=HD, j=HC),
                                             wq_raw[:, c, :].rearrange("p (k j d) -> p k d j", d=HD, j=HC),
                                             ACT.Copy).then_inc(wq_high, 1)
            act.wait_ge(job_freed, NJOB_A)
            for cyc, (u, kb) in enumerate(CYCLES):
                d = max(0, kb - TB * half_of(u))
                if cyc >= NP_BUF:
                    act.wait_ge(pv_done, cyc - NP_BUF + 1)
                for j in range(REP):
                    e = REP * cyc + j
                    act.wait_ge(scores, e + 1)
                    nc.scalar.activation(PB[:, cyc % NP_BUF, j, d * P:HT],
                                         PS[:, MAX_BANKS + e % ST_BANKS, 0:HT - d * P],
                                         ACT.Exp, scale=SCALE).then_inc(probs, 1)
                if kb == 0 and u:
                    evacuate(u - 1)
                kind, b, _ = job = FILL.get(cyc, ("", 0, 0))
                if job in JOB:
                    act_job(JOB[job])
                if kind == "T2":
                    context_high(b, MISC)
                if kind == "T3":
                    x1_high(b, MISC)
                if cyc in ROWS_AT:
                    turn_rows(ROWS_AT[cyc])
            evacuate(NU - 1)

            for kind, i in TAIL:
                if kind == "T2":
                    context_high(B0 + i, tail_bank(kind, i))
                if kind == "T3":
                    x1_high(B0 + i, tail_bank(kind, i))

        @block.vector
        def _(dve):
            step = [0]

            def link(ins):
                step[0] += 1
                ins.then_inc(dve_step, 1)
                dve.wait_ge(dve_step, step[0])

            def chunk_max(i, k):
                u, qb, j = item(i)
                n = chunks_before(i) + k
                part = MX[:, u % 2, i % ITEMS, :]
                bank = PS[:, n % MAX_BANKS, :]
                dve.wait_ge(max_scores, n + 1)
                if k < half_of(u):
                    nc.vector.tensor_reduce(part[:, 0:1], bank, AX, ALU.max).then_inc(max_read, 1)
                    return
                if qb:
                    nc.vector.tensor_reduce(part[:, 1:2], bank[:, 0:qb * P], AX, ALU.max)
                nc.vector.tensor_tensor_reduce(out=scrap[:, i % 4, :], in0=bank[:, qb * P:(qb + 1) * P],
                                               in1=mask[:, :], scale=1.0, scalar=LOWEST, op0=ALU.add,
                                               op1=ALU.max, accum_out=part[:, 2:3]).then_inc(max_read, 1)
                if i % ITEMS == ITEMS - 1:
                    finish_maxima(u, n + 1)

            def finish_maxima(u, chunks):
                par = u % 2

                def view(t):
                    return t.rearrange("p (q j) -> p q j", j=REP)
                dve.wait_ge(max_read, chunks)
                link(nc.vector.tensor_reduce(NM[:, par, :], MX[:, par, :, :], AX, ALU.max, negate=True))
                if u >= 2:
                    dve.wait_ge(nm_turned, u - 1)
                link(nc.vector.tensor_copy(NMP[:, par, :, 0, :], view(NM[:, par, :])))
                link(nc.vector.tensor_tensor(view(NM2[:, par, :]), view(NM[:, par, :]), NMP[:, par, :, 0, :],
                                             ALU.subtract))
                link(nc.vector.tensor_copy(NMP[:, par, :, 1, :], view(NM2[:, par, :])))
                nc.vector.tensor_tensor(NMP[:, par, :, 2, :], view(NM2[:, par, :]), NMP[:, par, :, 1, :],
                                        ALU.subtract).then_inc(nm_parts, 1)

            def dve_job(n):
                kind, h, c = JOBS[n]
                bank = job_bank(n)
                if kind in ("V", "bT"):
                    dve.wait_ge(job_done, n + 1)
                else:
                    dve.wait_ge(act_copied, sum(1 for j in JOBS[:n + 1] if j[0] not in ("V", "bT")))
                if kind == "xT":
                    half = slice(h * HT, (h + 1) * HT)
                    nc.vector.tensor_tensor(XT[:, 1, c, half], bank, XT[:, 0, c, half].bitcast(F32),
                                            ALU.subtract).then_inc(job_freed, 1)
                elif kind == "V":
                    nc.vector.tensor_copy(VX[:, h * TB:(h + 1) * TB, :, 0:HD],
                                          bank.rearrange("p (b g d) -> p b g d", b=TB, d=HD))\
                        .then_inc(job_freed, 1)
                elif kind in "KQ":
                    m = PROJ.index((kind, h, c))
                    s = m % 2
                    nc.vector.tensor_tensor(rest[:, s, :], bank, parts[:, s, 0, :], ALU.subtract)\
                        .then_inc(job_freed, 1)
                    dve.wait_ge(job_freed, n + 1)
                    nc.vector.tensor_copy(parts[:, s, 1, :], rest[:, s, :]).then_inc(rest_split, 1)
                elif kind == "bT":
                    nc.vector.tensor_scalar(bT, bank, LORA_SCALE, None, ALU.mult).then_inc(job_freed, 1)
                elif kind == "WE":
                    nc.vector.tensor_tensor(WEL[:, c, :], bank, WE[:, c, :].bitcast(F32), ALU.subtract)\
                        .then_inc(job_freed, 1)

            def normalise_context(b, k, bank):
                n = 2 * b + k
                dve.wait_ge(t1_done, n + 1)
                heads = PS[:, bank, :].rearrange("p (h e) -> p h e", e=2 * HD)
                if k == 0 and b >= 2:
                    dve.wait_ge(t2_done, b - 1)
                link(nc.vector.reciprocal(rec[:, n % 4, :], heads[:, :, HD]))
                nc.vector.tensor_tensor(CTX[b % 2][:, k * D // 2:(k + 1) * D // 2].rearrange("p (h d) -> p h d", d=HD),
                                        heads[:, :, 0:HD], rec[:, n % 4, :].unsqueeze(2)
                                        .broadcast_to([P, H // 2, HD]), ALU.mult).then_inc(ctx_ready, 1)

            def context_low(b, bank):
                dve.wait_ge(ct_hi, b + 1)
                nc.vector.tensor_tensor(CT[:, b % 2, 1, :, :], blocks(PS[:, bank, :]),
                                        CT[:, b % 2, 0, :, :].bitcast(F32), ALU.subtract).then_inc(ct_ready, 1)

            def x1_low(b, bank):
                dve.wait_ge(x1_hi, b + 1)
                nc.vector.tensor_tensor(X1T[:, b % 2, 1, :, :], blocks(PS[:, bank, :]),
                                        X1T[:, b % 2, 0, :, :].bitcast(F32), ALU.subtract).then_inc(x1t_ready, 1)

            norms = [0, 0]
            normed = [0, 0]

            def moments():
                s = norms[0] % 4
                norms[0] += 1
                link(nc.vector.bn_stats(stats[:, s, :], Y))
                link(nc.vector.bn_aggr(mv[:, s, :], stats[:, s, :]))
                nc.vector.tensor_scalar_add(mv[:, s, 1:2], mv[:, s, 1:2], EPS).then_inc(ln_var, 1)

            def scaled(result, ready):
                n = norms[1]
                norms[1] += 1
                s = n % 4
                dve.wait_ge(ln_root, n + 1)
                nc.vector.tensor_scalar(result, Y, mv[:, s, 0:1], rstd[:, s:s + 1], ALU.subtract, ALU.mult)\
                    .then_inc(ready, 1)

            def y_free():
                for ready, count in zip((x1_ready, out_ready), normed):
                    if count:
                        dve.wait_ge(ready, count)

            def first_residual(b, bank):
                y_free()
                dve.wait_ge(wo_done, b + 1)
                dve.wait_ge(xr_ready, b + 1)
                nc.vector.tensor_tensor(Y, PS[:, bank, :], X[:, b, :], ALU.add).then_inc(y1_read, 1)
                dve.wait_ge(y1_read, b + 1)
                moments()

            def first_norm(b):
                if b >= 2:
                    dve.wait_ge(x1b_ready, b - 1)
                    dve.wait_ge(t3_done, b - 1)
                scaled(X1[b % 2], x1_ready)
                normed[0] += 1

            def second_residual(b, bank):
                y_free()
                dve.wait_ge(ffn_done, b + 1)
                dve.wait_ge(x1b_ready, b + 1)
                nc.vector.tensor_tensor(Y, PS[:, bank, :], X1B[b % 2], ALU.add).then_inc(y2_read, 1)
                dve.wait_ge(y2_read, b + 1)
                moments()

            def second_norm(b):
                if b >= 2:
                    dve.wait_ge(out_done[b % 2], 16 * (b // 2))
                scaled(OUT[b % 2], out_ready)
                normed[1] += 1

            dve.wait_ge(wkv_in, 16)
            for c in range(NC):
                keys = wkv_v[:, c, 0, :, :].rearrange("p g d -> p d g")
                hi = WQ[:, 0, c, D:D + KD].rearrange("p (d g) -> p d g", g=G)
                lo = WQ[:, 1, c, D:D + KD].rearrange("p (d g) -> p d g", g=G)
                link(nc.vector.tensor_copy(hi, keys))
                nc.vector.tensor_tensor(lo, keys, hi.bitcast(F32), ALU.subtract).then_inc(wk_split, 1)
            issued = 0
            for n in range(NJOB_A):
                dve_job(n)
                while issued < early_items(n):
                    if issued == 0:
                        dve.wait_ge(consts, 3)
                    chunk_max(issued, 0)
                    issued += 1
            for i in range(issued, items_due(0)):
                chunk_max(i, 0)
            for cyc in range(NCYC):
                for lot in chunks_of_cycle(cyc):
                    for i, k in lot:
                        chunk_max(i, k)
                before = FILL.get(cyc - 1, ("", 0, 0))
                if before[0] == "WO":
                    first_norm(before[1])
                if before[0] == "FF":
                    second_norm(before[1])
                kind, b, _ = job = FILL.get(cyc, ("", 0, 0))
                if job in JOB:
                    dve_job(JOB[job])
                if kind in ("T1a", "T1b"):
                    normalise_context(b, int(kind == "T1b"), MISC)
                if kind == "T2":
                    context_low(b, MISC)
                if kind == "WO":
                    first_residual(b, MISC)
                if kind == "T3":
                    x1_low(b, MISC)
                if kind == "FF":
                    second_residual(b, MISC)
            for kind, i in TAIL_DVE:
                b = B0 + i
                if kind == "N1":
                    first_norm(b)
                elif kind == "N2":
                    second_norm(b)
                elif kind == "T1":
                    for k in range(2):
                        normalise_context(b, k, tail_bank(kind, i) + k)
                else:
                    {"T2": context_low, "WO": first_residual, "T3": x1_low, "FF": second_residual}[kind](
                        b, tail_bank(kind, i))

        @block.tensor
        def _(pe):
            def chunk_scores(i, k):
                u, qb, j = item(i)
                h, g = divmod(u, G)
                if i % ITEMS == 0 and k == 0:
                    pe.wait_ge(qs_in[u % SLOTS], 48 * (u // SLOTS + 1))
                    if u % G == 0:
                        pe.wait_ge(ks_in[h], 96)
                n = chunks_before(i) + k
                width = HT if k < h else (qb + 1) * P
                if n >= MAX_BANKS:
                    pe.wait_ge(max_read, n - MAX_BANKS + 1)
                nc.tensor.matmul(PS[:, n % MAX_BANKS, 0:width],
                                 QS[0:ROWS, u % SLOTS, j, qb * P:(qb + 1) * P],
                                 KS[0:ROWS, g, k * HT:k * HT + width], start=True, stop=True)\
                    .then_inc(max_scores, 1)

            def misc_free(job):
                k = MISC_ORDER.index(job)
                if k:
                    pe.wait_ge(*freed(MISC_ORDER[k - 1]))

            def turn_maxima(u):
                misc_free(("rows", u, 0))
                pe.wait_ge(nm_parts, u + 1)
                for qb in range(TB):
                    last = nc.tensor.matmul(PS[0:NPART * REP, MISC, qb * P:(qb + 1) * P],
                                            NMP[:, u % 2, qb, :, :].rearrange("p a j -> p (a j)"),
                                            ident_bf[:, :], start=True, stop=True)
                last.then_inc(nm_turned, 1)

            def third(part, count):
                return range(count * part // 3, count * (part + 1) // 3)

            def halves(bank, lhs, rhs, part):
                terms = [(c, a, b) for c in range(NC) for a, b in ((0, 0), (0, 1), (1, 0))]
                for k in third(part, len(terms)):
                    c, a, b = terms[k]
                    last = nc.tensor.matmul(bank, lhs(a, c), rhs(b, c), start=(k == 0), stop=(k == len(terms) - 1))
                return last

            def pe_job(n, part):
                kind, h, c = JOBS[n]
                bank = job_bank(n)
                half = slice(h * HT, (h + 1) * HT)
                if part == 0:
                    if n >= NJOB_A:
                        misc_free(JOBS[n])
                    elif n >= RING:
                        pe.wait_ge(job_freed, n - RING + 1)
                if kind == "xT":
                    if part == 0 and c == 0:
                        pe.wait_ge(x_in[h], 16)
                    for b in third(part, TB):
                        last = nc.tensor.transpose(bank[:, b * P:(b + 1) * P],
                                                   X[:, h * TB + b, c * P:(c + 1) * P], ident[:, :])
                elif kind == "V":
                    if part == 0:
                        pe.wait_ge(wkv_in, 16)
                        pe.wait_ge(xt32, NC * (h + 1))
                    for k in third(part, TB * NC):
                        b, cc = divmod(k, NC)
                        t0 = h * HT + b * P
                        last = nc.tensor.matmul(bank[:, b * P:(b + 1) * P], xT[:, cc, t0:t0 + P],
                                                wkv_v[:, cc, 1, :, :], start=(cc == 0), stop=(cc == NC - 1))
                elif kind == "K":
                    if part == 0:
                        pe.wait_ge(wk_split, NC)
                        pe.wait_ge(job_freed, JOB[("xT", h, NC - 1)] + 1)
                    last = halves(bank, lambda a, cc: WQ[:, a, cc, D:D + KD], lambda a, cc: XT[:, a, cc, half], part)
                elif kind == "Q":
                    if part == 0:
                        pe.wait_ge(wq_split, NC)
                        pe.wait_ge(job_freed, JOB[("xT", h, NC - 1)] + 1)
                    last = halves(bank, lambda a, cc: WQ[:, a, cc, c * P:(c + 1) * P],
                                  lambda a, cc: XT[:, a, cc, half], part)
                elif kind == "bT":
                    if part == 0:
                        pe.wait_ge(b_scaled, NC)
                    for cc in third(part, NC):
                        last = nc.tensor.transpose(bank[:, cc * P:(cc + 1) * P],
                                                   b_raw[:, cc, :, :].rearrange("p n r -> p (n r)"), ident[:, :])
                elif kind == "WE":
                    if part == 0:
                        pe.wait_ge(w_in, 16)
                        pe.wait_ge(job_freed, JOB[("bT", 0, 0)] + 1)
                    for k in third(part, 1 + NC):
                        o = k - 1
                        if k == 0:
                            last = nc.tensor.matmul(bank, a_raw[:, c * P:(c + 1) * P], bT, start=True, stop=False)
                        else:
                            last = nc.tensor.matmul(bank[:, o * P:(o + 1) * P], w_raw[:, o, c * P:(c + 1) * P],
                                                    ident[:, :], start=False, stop=(o == NC - 1))
                if part == 2:
                    last.then_inc(job_done, 1)

            def pe_step(kind, b, bank, part):
                h, qb = divmod(b, TB)
                bank = PS[:, bank, :]
                if kind in ("T1a", "T1b"):
                    g0 = 4 * int(kind == "T1b")
                    if part == 0:
                        pe.wait_ge(raw_out, h * G + g0 + 4)
                    for g in third(part, 4):
                        last = nc.tensor.transpose(bank[:, g * P:(g + 1) * P],
                                                   RAW[:, h * G + g0 + g, qb * P:(qb + 1) * P], ident[:, :])
                    done = t1_done
                elif kind in ("T2", "T3"):
                    if part == 0:
                        pe.wait_ge(*((ctx_ready, 2 * b + 2) if kind == "T2" else (x1_ready, b + 1)))
                    src = (CTX if kind == "T2" else X1)[b % 2]
                    for c in third(part, NC):
                        last = nc.tensor.transpose(bank[:, c * P:(c + 1) * P], src[:, c * P:(c + 1) * P],
                                                   ident[:, :])
                    done = t2_done if kind == "T2" else t3_done
                elif kind == "WO":
                    if part == 0:
                        pe.wait_ge(ct_ready, b + 1)
                        pe.wait_ge(wo_split, NC)
                    last = halves(bank, lambda a, c: CT[:, b % 2, a, c, :], lambda a, c: WQ[:, a, c, 0:D], part)
                    done = wo_done
                else:
                    if part == 0:
                        pe.wait_ge(x1t_ready, b + 1)
                        pe.wait_ge(job_freed, len(JOBS))
                    last = halves(bank, lambda a, c: X1T[:, b % 2, a, c, :],
                                  lambda a, c: (WEL if a else WE)[:, c, :], part)
                    done = ffn_done
                if part == 2:
                    last.then_inc(done, 1)

            pe.wait_ge(consts, 1)
            issued = 0
            for n in range(NJOB_A):
                if n == NJOB_A - 1:
                    turn_maxima(0)
                for part in range(3):
                    pe_job(n, part)
                    while issued < early_items(n) * (part + 1) // 3:
                        chunk_scores(issued, 0)
                        issued += 1
                while issued < early_items(n):
                    chunk_scores(issued, 0)
                    issued += 1
            for i in range(issued, items_due(0)):
                chunk_scores(i, 0)
            pe.wait_ge(job_freed, NJOB_A)
            pe.wait_ge(consts, 6)

            def filler(cyc, part):
                if cyc not in FILL:
                    return
                kind, b, _ = job = FILL[cyc]
                if job in JOB:
                    pe_job(JOB[job], part)
                else:
                    if part == 0:
                        misc_free(job)
                    pe_step(kind, b, MISC, part)

            def accumulate(cyc):
                u, kb = CYCLES[cyc]
                d = kb - TB * half_of(u)
                if d >= 0:
                    diag = sum(1 for v, k in CYCLES[:cyc + 1] if k >= TB * half_of(v))
                    pe.wait_ge(masked, 2 * diag)
                pe.wait_ge(probs, REP * (cyc + 1))
                d = max(d, 0)
                if kb == 0 and u:
                    pe.wait_ge(raw_out, u)
                n_kb = TB * (1 + half_of(u))
                for j in range(REP):
                    last = nc.tensor.matmul(PS[32 * j:32 * j + 32, PV_BANK, d * P:HT], VX[:, kb, u % G, :],
                                            PB[:, cyc % NP_BUF, j, d * P:HT], start=(kb == 0),
                                            stop=(kb == n_kb - 1))
                last.then_inc(pv_done, 1)

            def head_scores(cyc, j):
                u, kb = CYCLES[cyc]
                d = max(0, kb - TB * half_of(u))
                e = REP * cyc + j
                if e >= ST_BANKS:
                    pe.wait_ge(probs, e - ST_BANKS + 1)
                nc.tensor.matmul(PS[:, MAX_BANKS + e % ST_BANKS, 0:HT - d * P],
                                 KS[0:NROW, u % G, kb * P:(kb + 1) * P],
                                 QS[0:NROW, u % SLOTS, j, d * P:HT], start=True, stop=True)\
                    .then_inc(scores, 1)

            for cyc, (u, kb) in enumerate(CYCLES):
                if kb == 0:
                    pe.wait_ge(nm_in, 16 * (u + 1))
                for j, lot in enumerate(chunks_of_cycle(cyc)):
                    for i, k in lot:
                        chunk_scores(i, k)
                    head_scores(cyc, j)
                    if j % 2:
                        filler(cyc, j // 2)
                if cyc:
                    accumulate(cyc - 1)
                filler(cyc, 2)
                if cyc in ROWS_AT:
                    turn_maxima(ROWS_AT[cyc])
            accumulate(NCYC - 1)

            pe.wait_ge(max_read, chunks_before(ITEMS * NU))
            pe.wait_ge(probs, REP * NCYC)
            pe.wait_ge(*freed(MISC_ORDER[-1]))
            for kind, i in TAIL:
                b = B0 + i
                bank = tail_bank(kind, i)
                if kind == "T1":
                    for k, half in enumerate(("T1a", "T1b")):
                        if i >= 2:
                            pe.wait_ge(ctx_ready, 2 * (b - 2) + k + 1)
                        for part in range(3):
                            pe_step(half, b, bank + k, part)
                    continue
                if kind in ("T2", "T3") and i >= 2:
                    pe.wait_ge(*freed((kind, b - 2, 0)))
                if kind == "T3" and i < 2:
                    pe.wait_ge(*freed(("T2", b + 2, 0)))
                if kind == "WO" and i >= 2:
                    pe.wait_ge(*freed((kind, b - 2, 0)))
                if kind == "FF":
                    pe.wait_ge(ctx_ready, 2 * NT)
                for part in range(3):
                    pe_step(kind, b, bank, part)


_INS = ["L0_attn_x", "L0_attn_Wq", "L0_attn_Wkv", "L0_attn_Wo", "L0_attn_bo", "L0_ffn_lora_A", "L0_ffn_lora_B",
        "L0_ffn_W", "L0_ffn_bias", "L0_ffn_lora_weights"]
_OUTS = [((1, 1024, 512), "float32")]


def kernel(**inputs):
    import numpy as _np
    import concourse.bacc as _bacc
    from concourse import mybir as _mybir
    from concourse.bass_utils import run_bass_kernel_spmd as _run

    nc = _bacc.Bacc("TRN2", target_bir_lowering=False, num_devices=1)
    arrays, args = {}, []
    for name in _INS:
        a = _np.ascontiguousarray(inputs[name])
        arrays[f"in_{name}_dram"] = a
        args.append(nc.dram_tensor(f"in_{name}_dram", a.shape, _mybir.dt.from_np(a.dtype), kind="ExternalInput").ap())
    for i, (shape, dtype) in enumerate(_OUTS):
        dt = _mybir.dt.from_np(_np.dtype(dtype))
        args.append(nc.dram_tensor(f"out_{i}_dram", shape, dt, kind="ExternalOutput").ap())
    postln_kernel(nc, *args)
    r = _run(nc, [arrays], core_ids=[0])
    got = tuple(r.results[0][f"out_{i}_dram"] for i in range(len(_OUTS)))
    return got[0]
```

```python
import numpy as np
import concourse.bass as bass
from concourse import mybir
from contextlib import ExitStack

F32 = mybir.dt.float32
F32R = mybir.dt.float32r
BF16 = mybir.dt.bfloat16
ACT = mybir.ActivationFunctionType
ALU = mybir.AluOpType
AX = mybir.AxisListType.X

P = 128
LOWEST = -3.0e38
EPS = 1e-5
ONE_ONE = float(np.array([0x3F803F80], np.uint32).view(np.float32)[0])
ALPHA = 32


def postln_kernel(nc, x, wq, wkv, wo, bo, lora_a, lora_b, w, bias, lora_w, out):
    _, T, D = x.shape
    N_LORA, RANK, _ = lora_a.shape
    HD = 16
    H = D // HD
    G = wkv.shape[1] // (2 * HD)
    REP = H // G
    NC = D // P
    NT = T // P
    HT = T // 2
    TB = HT // P
    KD = G * HD
    HC = P // HD
    SCALE = 1.0 / HD ** 0.5
    LORA_SCALE = ALPHA / RANK
    assert KD == P and N_LORA * RANK == P and D == HT == 512 and REP == 4 and NC == TB == 4

    NPART = 3
    ROWS = 6 * HD
    NROW = ROWS + NPART

    NU = 2 * G
    CYCLES = [(u, kb) for u in range(NU) for kb in range(TB * (1 + u // G))]
    FIRST = [CYCLES.index((u, 0)) for u in range(NU)]
    NCYC = len(CYCLES)
    LEAD = 3
    SLOTS = 5
    NP_BUF = 3

    def half_of(u):
        return u // G

    def heads_per_bank(width):
        return min(REP, HT // width) if width <= HT // 2 else 1

    def heads_in_banks(width):
        n = heads_per_bank(width)
        return [range(j, j + n) for j in range(0, REP, n)]

    CHUNKS = []
    for u in range(NU):
        for qb in range(TB):
            if half_of(u):
                CHUNKS += [(u, qb, 0, range(j, j + 1)) for j in range(REP)]
            CHUNKS += [(u, qb, 1, heads) for heads in heads_in_banks((qb + 1) * P)]
    UNIT_CHUNKS = [sum(1 for ch in CHUNKS if ch[0] < u) for u in range(NU + 1)]

    def chunk_cost(ch):
        _, qb, own, heads = ch
        if not own:
            return 65 + HT
        return len(heads) * (65 + P) + (65 + len(heads) * qb * P if qb else 0)

    COST = [0]
    for ch in CHUNKS:
        COST.append(COST[-1] + chunk_cost(ch))

    def rows_cycle(u):
        return FIRST[u] - LEAD if u else -1

    ROWS_AT = {rows_cycle(u): u for u in range(1, NU)}

    def score_width(cyc):
        u, kb = CYCLES[cyc]
        return HT - max(0, kb - TB * half_of(u)) * P

    SCORE_BANKS = [0]
    for c in range(NCYC):
        SCORE_BANKS.append(SCORE_BANKS[-1] + len(heads_in_banks(score_width(c))))

    PLAN_A = [(("xT", 0, c), 0) for c in range(NC)]
    PLAN_A += [(("K", 0, 0), 0), (("Q", 0, 0), 0), (("V", 0, 0), 0), (("Q", 0, 1), 0), (("VT", 0, 0), 0)]
    PLAN_A += [(("xT", 1, c), 0) for c in range(NC)]
    PLAN_A += [(("Q", 0, 2), 5), (("K", 1, 0), 11), (("V", 1, 0), 15), (("Q", 0, 3), 20), (("VT", 1, 0), 22)]
    JOBS = [job for job, _ in PLAN_A]
    NJOB_A = len(JOBS)
    ROWS0_AFTER = 15
    LATER = [("Q", 1, c) for c in range(NC)] + [("bT", 0, 0)] + [("WE", 0, c) for c in range(NC)]
    JOBS += LATER
    JOB = {job: n for n, job in enumerate(JOBS)}
    RING = 4
    BLOCK_CYCLES = 15
    BY_ACT = ("V", "VT")
    PROJ = [j for j in JOBS if j[0] in ("K", "Q")]
    PROJ_A = sum(1 for j in JOBS[:NJOB_A] if j in PROJ)

    def chunks_of_job(n, part):
        before, due = PLAN_A[n - 1][1] if n else 0, PLAN_A[n][1]
        a, b = (before + (max(before, due) - before) * p // 3 for p in (part, part + 1))
        return range(a, b)

    def nth(job, kinds):
        return sum(1 for j in JOBS[:JOB[job] + 1] if j[0] in kinds)

    DVE_KINDS = ("xT", "K", "Q", "bT", "WE")
    HIGH_KINDS = ("xT", "K", "Q", "WE")

    STEPS = [(kind, b, 0) for b in range(TB) for kind in ("T1a", "T1b", "T2", "WO", "T3", "FF")]
    FILL = {2 * n: job for n, job in enumerate(LATER)}
    for n, job in enumerate(STEPS):
        b, k = divmod(n, 6)
        c = FIRST[G] + BLOCK_CYCLES * b + (0, 2, 4, 6, 9, 11)[k]
        FILL[c + 1 if c in ROWS_AT else c] = job
    assert len(FILL) == len(LATER + STEPS) and max(FILL) < NCYC - 2 and not set(FILL) & set(ROWS_AT)
    assert list(FILL) == sorted(FILL)

    POOL_AT = {c + 1: [("low", PROJ.index(job))] for c, job in FILL.items() if job in PROJ}
    for b in range(TB):
        POOL_AT.setdefault(4 * b + 9, []).append(("x", b))
        POOL_AT.setdefault(4 * b + 11, []).append(("wo", b))
        POOL_AT.setdefault(FIRST[G] + b, []).append(("x", TB + b))
        c = [c for c, job in FILL.items() if job == ("WO", b, 0)][0] + 2
        while (c - FIRST[G]) % (2 * TB) not in (0, 1, 2):
            c += 1
        POOL_AT.setdefault(c, []).append(("bias", b))

    WO_HIGH_AT = [4 * c + 9 for c in range(NC)]

    PE_FILL = {"T1a": 520, "T1b": 520, "T2": 520, "T3": 520, "bT": 520, "WE": 1700}
    DVE_FILL = {"T1a": 700, "T1b": 700, "T2": 600, "T3": 600, "bT": 600, "WE": 600, "Q": 950, "WO": 1850, "FF": 1850}

    def pe_time(c):
        kind = FILL[c][0] if c in FILL else None
        return REP * score_width(c) * (1 + 1.1) / 2.4 + (PE_FILL.get(kind, 2600) if kind else 0)

    def dve_time(c):
        return DVE_FILL[FILL[c - 1][0]] if c - 1 in FILL else 0

    def level(chunks, cycles):
        total = COST[chunks[-1] + 1] - COST[chunks[0]]
        low, high = 0.0, 9.0
        for _ in range(40):
            ratio = (low + high) / 2
            room = [max(0.0, 1000 * ratio - 0.5 * dve_time(c) + 0.2 * pe_time(c)) for c in cycles]
            low, high = (low, ratio) if sum(room) > total else (ratio, high)
        done, due = 0.0, []
        for r in room:
            done += r
            due.append(sum(1 for n in chunks if COST[n + 1] - COST[chunks[0]] <= done + 1))
        due[-1] = len(chunks)
        return [chunks[0] + d for d in due]

    START_UNITS = 2
    TURN = FIRST[G] - LEAD
    DUE = [UNIT_CHUNKS[START_UNITS]]
    DUE += level(range(UNIT_CHUNKS[START_UNITS], UNIT_CHUNKS[G + 1]), range(TURN))
    for u in range(G + 1, NU):
        DUE += level(range(UNIT_CHUNKS[u], UNIT_CHUNKS[u + 1]), range(FIRST[u - 1] - LEAD, FIRST[u] - LEAD))
    DUE += [len(CHUNKS)] * (NCYC + 1 - len(DUE))
    for u in range(1, NU):
        for c in range(rows_cycle(u), NCYC):
            DUE[c] = max(DUE[c], UNIT_CHUNKS[u + 1])

    def chunks_of_cycle(c):
        lot = range(DUE[c], DUE[c + 1])
        return [lot[len(lot) * q // 4:len(lot) * (q + 1) // 4] for q in range(4)]

    B0 = TB
    TAIL = [("T1", 0), ("T1", 1), ("T2", 0), ("T2", 1), ("T1", 2), ("WO", 0), ("T1", 3), ("T2", 2), ("WO", 1),
            ("T2", 3), ("WO", 2), ("T3", 0), ("WO", 3), ("T3", 1), ("FF", 0), ("T3", 2), ("FF", 1), ("T3", 3),
            ("FF", 2), ("FF", 3)]
    TAIL_DVE = [("T1", 0), ("T1", 1), ("T2", 0), ("T2", 1), ("T1", 2), ("WO", 0), ("T1", 3), ("N1", 0), ("T2", 2),
                ("WO", 1), ("T2", 3), ("N1", 1), ("WO", 2), ("T3", 0), ("N1", 2), ("WO", 3), ("T3", 1), ("N1", 3),
                ("FF", 0), ("T3", 2), ("N2", 0), ("FF", 1), ("T3", 3), ("N2", 1), ("FF", 2), ("N2", 2), ("FF", 3),
                ("N2", 3)]
    TAIL_POOL = [("root", 0), ("bias", 0), ("root", 1), ("bias", 1), ("root", 2), ("root", 3), ("root", 0),
                 ("bias", 2), ("root", 1), ("bias", 3), ("root", 2), ("root", 3)]

    def tail_bank(kind, i):
        return {"T1": 2 * (i % 2), "T2": 4 + i % 2, "T3": 4 + i % 2, "WO": 6 + i % 2, "FF": i}[kind]

    ctx = ExitStack()
    with ctx:
        def sb(name, shape, dt=F32):
            return ctx.enter_context(nc.sbuf_tensor(name, shape, dt))

        def sem(name):
            return ctx.enter_context(nc.semaphore(name))

        MAX_BANKS, ST_BANKS = 3, 3
        WIDE = SCORE_BANKS[rows_cycle(NU - 1) + 1]

        X = sb("X", [P, NT, D])
        RAW = sb("RAW", [P, NU, HT])
        wq_raw = RAW[:, G:G + 4, :]
        w_raw = RAW[:, G:G + 4, :]
        wo_raw = RAW[:, G + 4:G + 8, :]
        XT = sb("XT", [P, 2, NC, T], F32R)
        WE = XT[:, 0, :, 0:D]
        WEL = XT[:, 1, :, 0:D]
        CT = XT[:, :, :, D:D + 2 * P].rearrange("p a c (b t) -> p b a c t", b=2)
        X1T = XT[:, :, :, D + 2 * P:D + 4 * P].rearrange("p a c (b t) -> p b a c t", b=2)
        WQ = sb("WQ", [P, 2, NC, D + 2 * KD], F32R)
        QS = sb("QS", [P, SLOTS, REP, HT], BF16)
        KS = sb("KS", [P, G, T], BF16)
        VX = sb("VX", [P, NT, G, 2 * HD])
        PB = sb("PB", [P, NP_BUF, REP, HT])
        parts = sb("parts", [P, 2, NPART, HT], BF16)
        bias_bc = sb("bias_bc", [P, D])
        ident = sb("ident", [P, P])
        ident_bf = sb("ident_bf", [P, P], BF16)
        mask = sb("mask", [P, P])
        scrap = sb("scrap", [P, 2 * REP, P])
        coef = sb("coef", [P, N_LORA])
        MX = sb("MX", [P, 2, TB, REP, 3])
        NM = sb("NM", [P, 2, TB, REP])
        NM2 = sb("NM2", [P, 2, TB, REP])
        NMP = sb("NMP", [P, 2, TB, NPART, REP], BF16)
        NMR = sb("NMR", [P, 2, HT], BF16)
        stats = sb("stats", [P, 4, 6])
        mv = sb("mv", [P, 4, 2])
        minus_half = sb("minus_half", [P, 1])
        rstd = sb("rstd", [P, 4])
        rec = sb("rec", [P, 4, H // 2])

        TC = sb("TC", [P, 9, D])
        CTX = [TC[:, 0, :], TC[:, 1, :]]
        X1 = [TC[:, 2, :], TC[:, 3, :]]
        X1B = [TC[:, 4, :], TC[:, 5, :]]
        OUT = [TC[:, 6, :], TC[:, 7, :]]
        Y = TC[:, 8, :]
        a_raw, bT = TC[:, 0, :], TC[:, 8, :]
        b_raw = TC[:, 1, :].rearrange("p (c n r) -> p c n r", c=NC, n=N_LORA)
        wkv_raw = TC[:, 2:4, :].rearrange("p a n -> p (a n)").rearrange("p (c n) -> p c n", c=NC)
        wkv_v = wkv_raw.rearrange("p c (g two d) -> p c two g d", two=2, d=HD)
        bo_bc = TC[:, 4, :]
        vT = TC[:, 5, :]
        rest = TC[:, 6:8, :]

        PS = ctx.enter_context(nc.psum_tensor("PS", [P, 8, 512], F32))
        PV_BANK, MISC = 6, 7

        scr_q = nc.dram_tensor("scr_q", (2, NC, NPART, P, HT), BF16).ap()
        scr_k = nc.dram_tensor("scr_k", (2, NPART, KD, HT), BF16).ap()

        x_in = [[sem(f"x_in{h}{c}") for c in range(NC)] for h in range(2)]
        wkv_in, wq_in, ab_in, w_in, wo_in, bo_in = (sem(n) for n in (
            "wkv_in", "wq_in", "ab_in", "w_in", "wo_in", "bo_in"))
        consts = sem("consts")
        job_done = sem("job_done")
        job_freed = sem("job_freed")
        v_read = sem("v_read")
        act_copied = sem("act_copied")
        wk_split = sem("wk_split")
        wv_high, wv_split = sem("wv_high"), sem("wv_split")
        wq_high, wq_split = sem("wq_high"), sem("wq_split")
        b_scaled = sem("b_scaled")
        wo_high, wo_split = sem("wo_high"), sem("wo_split")
        rest_split = sem("rest_split")
        parts_ready = sem("parts_ready")
        parts_out = [sem(f"parts_out{b}") for b in range(2)]
        ks_in = [sem(f"ks_in{h}") for h in range(2)]
        qs_in = [sem(f"qs_in{s}") for s in range(SLOTS)]
        max_scores = sem("max_scores")
        max_read = sem("max_read")
        nm_parts = sem("nm_parts")
        nm_turned = sem("nm_turned")
        nm_rows = sem("nm_rows")
        nm_in = sem("nm_in")
        scores = sem("scores")
        probs = sem("probs")
        masked = sem("masked")
        pv_done = sem("pv_done")
        raw_out = sem("raw_out")
        xr_ready = sem("xr_ready")
        dve_step, pool_step = sem("dve_step"), sem("pool_step")
        t1_done, t2_done, wo_done, t3_done, ffn_done = (sem(n) for n in (
            "t1_done", "t2_done", "wo_done", "t3_done", "ffn_done"))
        ctx_ready, ct_hi, ct_ready = sem("ctx_ready"), sem("ct_hi"), sem("ct_ready")
        ln_var, ln_root = sem("ln_var"), sem("ln_root")
        y1_read, x1_ready, x1_hi, x1t_ready = (sem(n) for n in ("y1_read", "x1_ready", "x1_hi", "x1t_ready"))
        x1b_ready, y2_read, out_ready = sem("x1b_ready"), sem("y2_read"), sem("out_ready")
        out_done = [sem(f"out_done{b}") for b in range(2)]

        def score_bank(e):
            return MAX_BANKS + e % ST_BANKS if e < WIDE else (e - WIDE) % (MAX_BANKS + ST_BANKS)

        def job_bank(n):
            return PS[:, 3 + n % RING if n < NJOB_A else MISC, :]

        def freed(job):
            kind, b, _ = job
            if kind == "rows":
                return nm_rows, b + 1
            if kind in ("T1a", "T1b"):
                return ctx_ready, 2 * b + (2 if kind == "T1b" else 1)
            if kind in ("T2", "WO", "T3", "FF"):
                return {"T2": ct_ready, "WO": y1_read, "T3": x1t_ready, "FF": y2_read}[kind], b + 1
            if kind in BY_ACT:
                return v_read, nth(job, BY_ACT)
            return job_freed, nth(job, DVE_KINDS)

        MISC_ORDER = [("rows", 0, 0)] + [FILL[c] if c in FILL else ("rows", ROWS_AT[c], 0)
                                         for c in range(NCYC) if c in FILL or c in ROWS_AT]

        def blocks(bank):
            return bank.rearrange("p (c t) -> p c t", c=NC)

        def wq_part(half, k):
            return WQ[:, half, :, k * P:(k + 1) * P].rearrange("p c (d j) -> p c d j", d=HD)

        def wq_part_raw(k):
            return wq_raw[:, :, k * P:(k + 1) * P].rearrange("p c (j d) -> p c d j", d=HD)

        x_v = x.rearrange("a (h b p) d -> (a h) p b d", h=2, p=P)
        out_v = out.rearrange("a (b p) d -> (a b) p d", p=P)

        block = ctx.enter_context(nc.Block())

        @block.sync
        def _(sp):
            for c in range(NC):
                sp.dma_start(X[:, 0:TB, c * P:(c + 1) * P], x_v[0][:, :, c * P:(c + 1) * P]).then_inc(x_in[0][c], 16)
            sp.dma_start(wkv_raw, wkv.rearrange("(c p) n -> p c n", p=P)).then_inc(wkv_in, 16)
            sp.dma_start(wq_raw, wq.rearrange("(c p) n -> p c n", p=P)).then_inc(wq_in, 16)
            for c in range(NC):
                sp.dma_start(X[:, TB:NT, c * P:(c + 1) * P], x_v[1][:, :, c * P:(c + 1) * P]).then_inc(x_in[1][c], 16)
            sp.dma_start(bo_bc, bo.partition_broadcast(P)).then_inc(bo_in, 16)
            sp.dma_start(bias_bc[:, :], bias.partition_broadcast(P)).then_inc(bo_in, 16)

            def parts_to_dram(n):
                kind, h, c = PROJ[n]
                sp.wait_ge(parts_ready, n + 1)
                dst = scr_k[h] if kind == "K" else scr_q[h, c]
                sp.dma_start(dst.rearrange("a p t -> p a t"), parts[:, n % 2, :, :])\
                    .then_inc(parts_out[n % 2], 16)

            def parts_landed(n):
                sp.wait_ge(parts_out[n % 2], 16 * (n // 2 + 1))

            def load_keys(h):
                parts_landed(PROJ.index(("K", h, 0)))
                row = 0
                for a, copies in enumerate((3, 2, 1)):
                    sp.dma_start(KS[row:row + copies * HD, :, h * HT:(h + 1) * HT],
                                 scr_k[h, a].rearrange("(d g) t -> d g t", g=G).unsqueeze(0)
                                 .broadcast_to([copies, HD, G, HT])).then_inc(ks_in[h], 16)
                    row += copies * HD

            def load_queries(u):
                h, g = divmod(u, G)
                slot = u % SLOTS
                c, j0 = divmod(g * REP, HC)
                if u >= SLOTS:
                    sp.wait_ge(scores, SCORE_BANKS[FIRST[u - SLOTS + 1]])
                parts_landed(PROJ.index(("Q", h, c)))
                row = 0
                for run in (3, 2, 1):
                    sp.dma_start(QS[row:row + run * HD, slot, :, :],
                                 scr_q[h, c, 0:run].rearrange("a (d j) t -> (a d) j t", j=HC)[:, j0:j0 + REP, :])\
                        .then_inc(qs_in[slot], 16)
                    row += run * HD

            def move_maxima(u):
                sp.wait_ge(nm_rows, u + 1)
                for a in range(NPART):
                    sp.dma_start(QS[ROWS + a:ROWS + a + 1, u % SLOTS, :, :], NMR[a * REP:(a + 1) * REP, u % 2, :])\
                        .then_inc(nm_in, 16)

            def store(b):
                sp.wait_ge(out_ready, b + 1)
                sp.dma_start(out_v[b], OUT[b % 2]).then_inc(out_done[b % 2], 16)

            for n in range(PROJ_A):
                if JOB[PROJ[n]] == ROWS0_AFTER + 1:
                    move_maxima(0)
                parts_to_dram(n)
                if n == 1:
                    load_keys(0)
                    load_queries(0)
                    load_queries(1)
                if n == 2:
                    sp.dma_start(wo_raw, wo.rearrange("(c p) n -> p c n", p=P)).then_inc(wo_in, 16)
                    sp.wait_ge(wq_split, NC)
                    sp.dma_start(w_raw, w.rearrange("(c p) n -> p c n", p=P)).then_inc(w_in, 16)
                    sp.dma_start(a_raw, lora_a.rearrange("n r d -> (n r) d")).then_inc(ab_in, 16)
                    for c in range(NC):
                        sp.dma_start(b_raw[:, c, :, :], lora_b[:, c * P:(c + 1) * P, :]
                                     .rearrange("n p r -> p n r")).then_inc(ab_in, 16)
                    sp.dma_start(coef[:, :], lora_w.partition_broadcast(P)).then_inc(ab_in, 16)
                if n == 3:
                    load_queries(2)
                    load_queries(3)
                if n == 4:
                    load_queries(4)
            load_keys(1)
            for cyc, (u, kb) in enumerate(CYCLES):
                if kb == 0 and 1 <= u and u + SLOTS - 1 < NU:
                    load_queries(u + SLOTS - 1)
                if FILL.get(cyc) in PROJ:
                    parts_to_dram(PROJ.index(FILL[cyc]))
                if cyc in ROWS_AT:
                    move_maxima(ROWS_AT[cyc])
                if cyc - 1 in FILL and FILL[cyc - 1][0] == "FF":
                    store(FILL[cyc - 1][1])
            for b in range(TB, NT):
                store(b)
            for s in range(2):
                sp.wait_ge(out_done[s], 16 * (NT // 2))

        @block.gpsimd
        def _(pool):
            step = [0]

            def link(ins):
                step[0] += 1
                ins.then_inc(pool_step, 1)
                pool.wait_ge(pool_step, step[0])

            def constant(ins, n):
                ins.then_inc(consts, 1)
                pool.wait_ge(consts, n)

            def low_part(n):
                pool.wait_ge(rest_split, n + 1)
                s = n % 2
                nc.gpsimd.tensor_tensor(parts[:, s, 2, :], rest[:, s, :], parts[:, s, 1, :], ALU.subtract)\
                    .then_inc(parts_ready, 1)

            link(nc.gpsimd.memset(ident[:, :], 0.0))
            constant(nc.gpsimd.affine_select(out=ident[:, :], in_=ident[:, :], compare_op=ALU.not_equal, fill=1.0,
                                             base=0, pattern=[[-1, P]], channel_multiplier=1), 1)
            link(nc.gpsimd.memset(mask[:, :], 0.0))
            constant(nc.gpsimd.affine_select(out=mask[:, :], in_=mask[:, :], compare_op=ALU.is_ge, fill=LOWEST,
                                             base=0, pattern=[[-1, P]], channel_multiplier=1), 2)
            constant(nc.gpsimd.memset(MX[:, :, :, :], LOWEST), 3)
            constant(nc.gpsimd.tensor_copy(ident_bf[:, :], ident[:, :]), 4)
            link(nc.gpsimd.memset(minus_half[:, :], -0.5))

            def wq_low(k):
                pool.wait_ge(wq_high, k + 1)
                nc.gpsimd.tensor_tensor(wq_part(1, k), wq_part_raw(k), wq_part(0, k).bitcast(F32),
                                        ALU.subtract).then_inc(wq_split, 1)

            wq_low(0)
            wq_low(1)
            wq_low(2)
            wq_low(3)
            constant(nc.gpsimd.memset(VX[:, :, :, HD:2 * HD], 1.0), 5)
            constant(nc.gpsimd.memset(KS[ROWS:NROW, :, :].rearrange("p g t -> p (g t)").bitcast(F32), ONE_ONE), 6)
            for n in range(2, PROJ_A):
                low_part(n)
            pool.wait_ge(ab_in, 16 * (NC + 2))
            for c in range(NC):
                nc.gpsimd.tensor_tensor(b_raw[:, c, :, :], b_raw[:, c, :, :],
                                        coef[:, :].unsqueeze(2).broadcast_to([P, N_LORA, RANK]),
                                        ALU.mult).then_inc(b_scaled, 1)
            pool.wait_ge(bo_in, 32)

            def residual_input(b):
                pool.wait_ge(job_done, JOB[("xT", 1, NC - 1)] + 1)
                nc.gpsimd.tensor_tensor(X[:, b, :], X[:, b, :], bo_bc, ALU.add).then_inc(xr_ready, 1)

            def split_wo(c):
                pool.wait_ge(wo_high, c + 1)
                nc.gpsimd.tensor_tensor(WQ[:, 1, c, 0:D], wo_raw[:, c, :], WQ[:, 0, c, 0:D].bitcast(F32),
                                        ALU.subtract).then_inc(wo_split, 1)

            roots = [0]

            def root():
                n = roots[0]
                roots[0] += 1
                pool.wait_ge(ln_var, n + 1)
                nc.gpsimd.tensor_tensor(rstd[:, n % 4:n % 4 + 1], mv[:, n % 4, 1:2], minus_half[:, 0:1], ALU.pow)\
                    .then_inc(ln_root, 1)

            def add_bias(b):
                pool.wait_ge(x1_ready, b + 1)
                if b >= 2:
                    pool.wait_ge(y2_read, b - 1)
                nc.gpsimd.tensor_tensor(X1B[b % 2], X1[b % 2], bias_bc[:, :], ALU.add).then_inc(x1b_ready, 1)

            for cyc, (u, kb) in enumerate(CYCLES):
                d = kb - TB * half_of(u)
                if d >= 0:
                    for pair in range(2):
                        pool.wait_ge(probs, SCORE_BANKS[cyc] + -(-(2 * pair + 2) // heads_per_bank(score_width(cyc))))
                        blk = PB[:, cyc % NP_BUF, 2 * pair:2 * pair + 2, d * P:(d + 1) * P]
                        nc.gpsimd.affine_select(out=blk, in_=blk, compare_op=ALU.is_ge, fill=0.0, base=0,
                                                pattern=[[0, 2], [1, P]], channel_multiplier=-1)\
                            .then_inc(masked, 1)
                        if pair == 0 and cyc - 1 in FILL and FILL[cyc - 1][0] in ("WO", "FF"):
                            root()
                elif cyc - 1 in FILL and FILL[cyc - 1][0] in ("WO", "FF"):
                    root()
                for job in POOL_AT.get(cyc, []):
                    {"low": low_part, "x": residual_input, "wo": split_wo, "bias": add_bias}[job[0]](job[1])
            for kind, i in TAIL_POOL:
                if kind == "root":
                    root()
                else:
                    add_bias(B0 + i)

        @block.scalar
        def _(act):
            def act_job(n):
                kind, h, c = JOBS[n]
                if kind == "bT":
                    return
                act.wait_ge(job_done, n + 1)
                if kind == "V":
                    nc.scalar.activation(vT, job_bank(n), ACT.Copy).then_inc(v_read, 1)
                elif kind == "VT":
                    nc.scalar.activation(VX[:, h * TB:(h + 1) * TB, :, 0:HD],
                                         job_bank(n).rearrange("p (b g d) -> p b g d", b=TB, d=HD), ACT.Copy)\
                        .then_inc(v_read, 1)
                elif kind == "xT":
                    half = slice(h * HT, (h + 1) * HT)
                    nc.scalar.activation(XT[:, 0, c, half], job_bank(n), ACT.Copy).then_inc(act_copied, 1)
                elif kind == "WE":
                    nc.scalar.activation(WE[:, c, :], job_bank(n), ACT.Copy).then_inc(act_copied, 1)
                else:
                    m = PROJ.index((kind, h, c))
                    if m >= 2:
                        act.wait_ge(parts_out[m % 2], 16 * (m // 2))
                    nc.scalar.activation(parts[:, m % 2, 0, :], job_bank(n), ACT.Copy).then_inc(act_copied, 1)

            def middle_part(n):
                act.wait_ge(*freed(PROJ[n]))
                nc.scalar.activation(parts[:, n % 2, 1, :], rest[:, n % 2, :], ACT.Copy).then_inc(rest_split, 1)

            def turn_rows(u):
                act.wait_ge(nm_turned, u + 1)
                if u >= 2:
                    act.wait_ge(nm_in, 16 * NPART * (u - 1))
                nc.scalar.activation(NMR[0:NPART * REP, u % 2, :], PS[0:NPART * REP, MISC, :], ACT.Copy)\
                    .then_inc(nm_rows, 1)

            def evacuate(u):
                last = FIRST[u + 1] if u + 1 < NU else NCYC
                act.wait_ge(pv_done, last)
                if u >= G + 4:
                    act.wait_ge(wo_split, NC)
                nc.scalar.activation(RAW[:, u, :], PS[:, PV_BANK, :], ACT.Copy).then_inc(raw_out, 1)

            def context_high(b, bank):
                act.wait_ge(t2_done, b + 1)
                if b >= 2:
                    act.wait_ge(wo_done, b - 1)
                nc.scalar.activation(CT[:, b % 2, 0, :, :], blocks(PS[:, bank, :]), ACT.Copy).then_inc(ct_hi, 1)

            def x1_high(b, bank):
                act.wait_ge(t3_done, b + 1)
                if b >= 2:
                    act.wait_ge(ffn_done, b - 1)
                nc.scalar.activation(X1T[:, b % 2, 0, :, :], blocks(PS[:, bank, :]), ACT.Copy).then_inc(x1_hi, 1)

            def wq_high_half(k):
                act.wait_ge(wq_in, 16)
                nc.scalar.activation(wq_part(0, k), wq_part_raw(k), ACT.Copy).then_inc(wq_high, 1)

            def wo_high_half(c):
                act.wait_ge(wo_in, 16)
                act.wait_ge(job_done, JOB[("Q", 1, NC - 1)] + 1)
                nc.scalar.activation(WQ[:, 0, c, 0:D], wo_raw[:, c, :], ACT.Copy).then_inc(wo_high, 1)

            for n in range(NJOB_A):
                act_job(n)
                if JOBS[n] in PROJ:
                    middle_part(PROJ.index(JOBS[n]))
                if n == NC - 1:
                    act.wait_ge(wkv_in, 16)
                    nc.scalar.activation(WQ[:, 0, :, D + KD:D + 2 * KD].rearrange("p c (g d) -> p c g d", d=HD),
                                         wkv_v[:, :, 1, :, :], ACT.Copy).then_inc(wv_high, 1)
                    wq_high_half(0)
                    wq_high_half(1)
                if n == NC + 1:
                    wq_high_half(2)
                    wq_high_half(3)
                if n == ROWS0_AFTER:
                    turn_rows(0)
            for cyc, (u, kb) in enumerate(CYCLES):
                d = max(0, kb - TB * half_of(u))
                if cyc >= NP_BUF:
                    act.wait_ge(pv_done, cyc - NP_BUF + 1)
                for k, heads in enumerate(heads_in_banks(HT - d * P)):
                    e = SCORE_BANKS[cyc] + k
                    act.wait_ge(scores, e + 1)
                    nc.scalar.activation(PB[:, cyc % NP_BUF, heads[0]:heads[-1] + 1, d * P:HT],
                                         PS[:, score_bank(e), 0:len(heads) * (HT - d * P)]
                                         .rearrange("p (j t) -> p j t", j=len(heads)),
                                         ACT.Exp, scale=SCALE).then_inc(probs, 1)
                if kb == 0 and u:
                    evacuate(u - 1)
                kind, b, _ = job = FILL.get(cyc, ("", 0, 0))
                if job in JOB:
                    act_job(JOB[job])
                if FILL.get(cyc - 1) in PROJ:
                    middle_part(PROJ.index(FILL[cyc - 1]))
                if kind == "T2":
                    context_high(b, MISC)
                if kind == "T3":
                    x1_high(b, MISC)
                if cyc in ROWS_AT:
                    turn_rows(ROWS_AT[cyc])
                if cyc in WO_HIGH_AT:
                    wo_high_half(WO_HIGH_AT.index(cyc))
            evacuate(NU - 1)

            for kind, i in TAIL:
                if kind == "T2":
                    context_high(B0 + i, tail_bank(kind, i))
                if kind == "T3":
                    x1_high(B0 + i, tail_bank(kind, i))

        @block.vector
        def _(dve):
            step = [0]

            def link(ins):
                step[0] += 1
                ins.then_inc(dve_step, 1)
                dve.wait_ge(dve_step, step[0])

            turn = [0]

            def chunk_max(n):
                u, qb, own, heads = CHUNKS[n]
                j0, j1 = heads[0], heads[-1] + 1
                part = MX[:, u % 2, qb, :, :]
                bank = PS[:, n % MAX_BANKS, :]
                dve.wait_ge(max_scores, n + 1)
                if not own:
                    nc.vector.tensor_reduce(part[:, j0:j1, 0:1], bank, AX, ALU.max).then_inc(max_read, 1)
                    return
                width = (qb + 1) * P
                bank = bank[:, 0:len(heads) * width].rearrange("p (j t) -> p j t", t=width)
                if qb:
                    nc.vector.tensor_reduce(part[:, j0:j1, 1:2], bank[:, :, 0:qb * P], AX, ALU.max)
                for j in heads:
                    turn[0] = (turn[0] + 1) % (2 * REP)
                    last = nc.vector.tensor_tensor_reduce(
                        out=scrap[:, turn[0], :], in0=bank[:, j - j0, qb * P:width], in1=mask[:, :], scale=1.0,
                        scalar=LOWEST, op0=ALU.add, op1=ALU.max, accum_out=part[:, j, 2:3])
                last.then_inc(max_read, 1)
                if n + 1 == UNIT_CHUNKS[u + 1]:
                    finish_maxima(u)

            def finish_maxima(u):
                par = u % 2
                dve.wait_ge(max_read, UNIT_CHUNKS[u + 1])
                link(nc.vector.tensor_reduce(NM[:, par, :, :], MX[:, par, :, :, :], AX, ALU.max, negate=True))
                if u >= 2:
                    dve.wait_ge(nm_turned, u - 1)
                link(nc.vector.tensor_copy(NMP[:, par, :, 0, :], NM[:, par, :, :]))
                link(nc.vector.tensor_tensor(NM2[:, par, :, :], NM[:, par, :, :], NMP[:, par, :, 0, :],
                                             ALU.subtract))
                link(nc.vector.tensor_copy(NMP[:, par, :, 1, :], NM2[:, par, :, :]))
                nc.vector.tensor_tensor(NMP[:, par, :, 2, :], NM2[:, par, :, :], NMP[:, par, :, 1, :],
                                        ALU.subtract).then_inc(nm_parts, 1)

            def dve_job(n):
                kind, h, c = JOBS[n]
                bank = job_bank(n)
                if kind in BY_ACT:
                    return
                if kind == "bT":
                    dve.wait_ge(job_done, n + 1)
                else:
                    dve.wait_ge(act_copied, nth(JOBS[n], HIGH_KINDS))
                if kind == "xT":
                    half = slice(h * HT, (h + 1) * HT)
                    nc.vector.tensor_tensor(XT[:, 1, c, half], bank, XT[:, 0, c, half].bitcast(F32),
                                            ALU.subtract).then_inc(job_freed, 1)
                elif kind in ("K", "Q"):
                    m = PROJ.index((kind, h, c))
                    s = m % 2
                    nc.vector.tensor_tensor(rest[:, s, :], bank, parts[:, s, 0, :], ALU.subtract)\
                        .then_inc(job_freed, 1)
                    if m < 2:
                        dve.wait_ge(rest_split, m + 1)
                        dve.wait_ge(*freed(JOBS[n]))
                        nc.vector.tensor_tensor(parts[:, s, 2, :], rest[:, s, :], parts[:, s, 1, :], ALU.subtract)\
                            .then_inc(parts_ready, 1)
                elif kind == "bT":
                    nc.vector.tensor_scalar(bT, bank, LORA_SCALE, None, ALU.mult).then_inc(job_freed, 1)
                elif kind == "WE":
                    nc.vector.tensor_tensor(WEL[:, c, :], bank, WE[:, c, :].bitcast(F32), ALU.subtract)\
                        .then_inc(job_freed, 1)

            def normalise_context(b, k, bank):
                n = 2 * b + k
                dve.wait_ge(t1_done, n + 1)
                heads = PS[:, bank, :].rearrange("p (h e) -> p h e", e=2 * HD)
                if k == 0 and b >= 2:
                    dve.wait_ge(t2_done, b - 1)
                link(nc.vector.reciprocal(rec[:, n % 4, :], heads[:, :, HD]))
                nc.vector.tensor_tensor(CTX[b % 2][:, k * D // 2:(k + 1) * D // 2].rearrange("p (h d) -> p h d", d=HD),
                                        heads[:, :, 0:HD], rec[:, n % 4, :].unsqueeze(2)
                                        .broadcast_to([P, H // 2, HD]), ALU.mult).then_inc(ctx_ready, 1)

            def context_low(b, bank):
                dve.wait_ge(ct_hi, b + 1)
                nc.vector.tensor_tensor(CT[:, b % 2, 1, :, :], blocks(PS[:, bank, :]),
                                        CT[:, b % 2, 0, :, :].bitcast(F32), ALU.subtract).then_inc(ct_ready, 1)

            def x1_low(b, bank):
                dve.wait_ge(x1_hi, b + 1)
                nc.vector.tensor_tensor(X1T[:, b % 2, 1, :, :], blocks(PS[:, bank, :]),
                                        X1T[:, b % 2, 0, :, :].bitcast(F32), ALU.subtract).then_inc(x1t_ready, 1)

            norms = [0, 0]
            residuals, normed = [0, 0], [0, 0]

            def moments():
                s = norms[0] % 4
                for read, count in zip((y1_read, y2_read), residuals):
                    if count:
                        dve.wait_ge(read, count)
                norms[0] += 1
                link(nc.vector.bn_stats(stats[:, s, :], Y))
                link(nc.vector.bn_aggr(mv[:, s, :], stats[:, s, :]))
                nc.vector.tensor_scalar_add(mv[:, s, 1:2], mv[:, s, 1:2], EPS).then_inc(ln_var, 1)

            def scaled(result, ready):
                n = norms[1]
                norms[1] += 1
                s = n % 4
                dve.wait_ge(ln_root, n + 1)
                nc.vector.tensor_scalar(result, Y, mv[:, s, 0:1], rstd[:, s:s + 1], ALU.subtract, ALU.mult)\
                    .then_inc(ready, 1)

            def y_free():
                for ready, count in zip((x1_ready, out_ready), normed):
                    if count:
                        dve.wait_ge(ready, count)

            def first_residual(b, bank):
                y_free()
                dve.wait_ge(wo_done, b + 1)
                dve.wait_ge(xr_ready, b + 1)
                nc.vector.tensor_tensor(Y, PS[:, bank, :], X[:, b, :], ALU.add).then_inc(y1_read, 1)
                residuals[0] += 1

            def first_norm(b):
                if b >= 2:
                    dve.wait_ge(x1b_ready, b - 1)
                    dve.wait_ge(t3_done, b - 1)
                scaled(X1[b % 2], x1_ready)
                normed[0] += 1

            def second_residual(b, bank):
                y_free()
                dve.wait_ge(ffn_done, b + 1)
                dve.wait_ge(x1b_ready, b + 1)
                nc.vector.tensor_tensor(Y, PS[:, bank, :], X1B[b % 2], ALU.add).then_inc(y2_read, 1)
                residuals[1] += 1

            def second_norm(b):
                if b >= 2:
                    dve.wait_ge(out_done[b % 2], 16 * (b // 2))
                scaled(OUT[b % 2], out_ready)
                normed[1] += 1

            for n in range(NJOB_A):
                for part in range(3):
                    if part == 2:
                        dve_job(n)
                    for k in chunks_of_job(n, part):
                        if k == 0:
                            dve.wait_ge(consts, 3)
                        chunk_max(k)
                if n == NC - 1:
                    dve.wait_ge(wkv_in, 16)
                    keys = wkv_v[:, :, 0, :, :].rearrange("p c g d -> p c d g")
                    hi, lo = (WQ[:, a, :, D:D + KD].rearrange("p c (d g) -> p c d g", g=G) for a in range(2))
                    link(nc.vector.tensor_copy(hi, keys))
                    nc.vector.tensor_tensor(lo, keys, hi.bitcast(F32), ALU.subtract).then_inc(wk_split, 1)
                    dve.wait_ge(wv_high, 1)
                    hi, lo = (WQ[:, a, :, D + KD:D + 2 * KD].rearrange("p c (g d) -> p c g d", d=HD)
                              for a in range(2))
                    nc.vector.tensor_tensor(lo, wkv_v[:, :, 1, :, :], hi.bitcast(F32), ALU.subtract)\
                        .then_inc(wv_split, 1)
            for cyc in range(NCYC):
                kind, b, _ = job = FILL.get(cyc - 1, ("", 0, 0))
                kind2, b2, _ = FILL.get(cyc - 2, ("", 0, 0))
                if kind2 == "WO":
                    first_norm(b2)
                if kind2 == "FF":
                    second_norm(b2)
                if kind in ("T1a", "T1b"):
                    normalise_context(b, int(kind == "T1b"), MISC)
                if kind == "WO":
                    first_residual(b, MISC)
                if kind == "FF":
                    second_residual(b, MISC)
                for q, lot in enumerate(chunks_of_cycle(cyc)):
                    for n in lot:
                        chunk_max(n)
                    if q == 0:
                        if job in JOB:
                            dve_job(JOB[job])
                        if kind == "T2":
                            context_low(b, MISC)
                        if kind == "T3":
                            x1_low(b, MISC)
                        if kind in ("WO", "FF"):
                            moments()
            for kind, i in TAIL_DVE:
                b = B0 + i
                if kind == "N1":
                    first_norm(b)
                elif kind == "N2":
                    second_norm(b)
                elif kind == "T1":
                    for k in range(2):
                        normalise_context(b, k, tail_bank(kind, i) + k)
                else:
                    {"T2": context_low, "WO": first_residual, "T3": x1_low, "FF": second_residual}[kind](
                        b, tail_bank(kind, i))
                    if kind in ("WO", "FF"):
                        moments()

        @block.tensor
        def _(pe):
            def chunk_scores(n):
                u, qb, own, heads = CHUNKS[n]
                h, g = divmod(u, G)
                if n == UNIT_CHUNKS[u]:
                    pe.wait_ge(qs_in[u % SLOTS], 48 * (u // SLOTS + 1))
                    if u % G == 0:
                        pe.wait_ge(ks_in[h], 48)
                width = (qb + 1) * P if own else HT
                k0 = h * HT if own else 0
                if n >= MAX_BANKS:
                    pe.wait_ge(max_read, n - MAX_BANKS + 1)
                for k, j in enumerate(heads):
                    last = nc.tensor.matmul(PS[:, n % MAX_BANKS, k * width:(k + 1) * width],
                                            QS[0:ROWS, u % SLOTS, j, qb * P:(qb + 1) * P],
                                            KS[0:ROWS, g, k0:k0 + width], start=True, stop=True)
                last.then_inc(max_scores, 1)

            def misc_free(job):
                k = MISC_ORDER.index(job)
                if k:
                    pe.wait_ge(*freed(MISC_ORDER[k - 1]))

            def turn_maxima(u):
                misc_free(("rows", u, 0))
                pe.wait_ge(nm_parts, u + 1)
                for qb in range(TB):
                    last = nc.tensor.matmul(PS[0:NPART * REP, MISC, qb * P:(qb + 1) * P],
                                            NMP[:, u % 2, qb, :, :].rearrange("p a j -> p (a j)"),
                                            ident_bf[:, :], start=True, stop=True)
                last.then_inc(nm_turned, 1)

            def third(part, count):
                return range(count * part // 3, count * (part + 1) // 3)

            def halves(bank, lhs, rhs, part):
                terms = [(c, a, b) for c in range(NC) for a, b in ((0, 0), (0, 1), (1, 0))]
                for k in third(part, len(terms)):
                    c, a, b = terms[k]
                    last = nc.tensor.matmul(bank, lhs(a, c), rhs(b, c), start=(k == 0), stop=(k == len(terms) - 1))
                return last

            def pe_job(n, part):
                kind, h, c = JOBS[n]
                bank = job_bank(n)
                half = slice(h * HT, (h + 1) * HT)
                if part == 0:
                    if n >= NJOB_A:
                        misc_free(JOBS[n])
                    elif n >= RING:
                        pe.wait_ge(*freed(JOBS[n - RING]))
                if kind == "xT":
                    if part == 0:
                        pe.wait_ge(x_in[h][c], 16)
                    for b in third(part, TB):
                        last = nc.tensor.transpose(bank[:, b * P:(b + 1) * P],
                                                   X[:, h * TB + b, c * P:(c + 1) * P], ident[:, :])
                elif kind in ("K", "V", "Q"):
                    if part == 0:
                        pe.wait_ge(*{"K": (wk_split, 1), "V": (wv_split, 1), "Q": (wq_split, c + 1)}[kind])
                        pe.wait_ge(*freed(("xT", h, NC - 1)))
                    col = {"K": D, "V": D + KD, "Q": c * P}[kind]
                    last = halves(bank, lambda a, cc: WQ[:, a, cc, col:col + P],
                                  lambda a, cc: XT[:, a, cc, half], part)
                elif kind == "VT":
                    if part == 0:
                        pe.wait_ge(*freed(("V", h, 0)))
                    for b in third(part, TB):
                        last = nc.tensor.transpose(bank[:, b * P:(b + 1) * P], vT[:, b * P:(b + 1) * P], ident[:, :])
                elif kind == "bT":
                    if part == 0:
                        pe.wait_ge(b_scaled, NC)
                    for cc in third(part, NC):
                        last = nc.tensor.transpose(bank[:, cc * P:(cc + 1) * P],
                                                   b_raw[:, cc, :, :].rearrange("p n r -> p (n r)"), ident[:, :])
                elif kind == "WE":
                    if part == 0:
                        pe.wait_ge(w_in, 16)
                        pe.wait_ge(*freed(("bT", 0, 0)))
                    for k in third(part, 1 + NC):
                        o = k - 1
                        if k == 0:
                            last = nc.tensor.matmul(bank, a_raw[:, c * P:(c + 1) * P], bT, start=True, stop=False)
                        else:
                            last = nc.tensor.matmul(bank[:, o * P:(o + 1) * P], w_raw[:, o, c * P:(c + 1) * P],
                                                    ident[:, :], start=False, stop=(o == NC - 1))
                if part == 2:
                    last.then_inc(job_done, 1)

            def pe_step(kind, b, bank, part):
                h, qb = divmod(b, TB)
                bank = PS[:, bank, :]
                if kind in ("T1a", "T1b"):
                    g0 = 4 * int(kind == "T1b")
                    if part == 0:
                        pe.wait_ge(raw_out, h * G + g0 + 4)
                    for g in third(part, 4):
                        last = nc.tensor.transpose(bank[:, g * P:(g + 1) * P],
                                                   RAW[:, h * G + g0 + g, qb * P:(qb + 1) * P], ident[:, :])
                    done = t1_done
                elif kind in ("T2", "T3"):
                    if part == 0:
                        pe.wait_ge(*((ctx_ready, 2 * b + 2) if kind == "T2" else (x1_ready, b + 1)))
                    src = (CTX if kind == "T2" else X1)[b % 2]
                    for c in third(part, NC):
                        last = nc.tensor.transpose(bank[:, c * P:(c + 1) * P], src[:, c * P:(c + 1) * P],
                                                   ident[:, :])
                    done = t2_done if kind == "T2" else t3_done
                elif kind == "WO":
                    if part == 0:
                        pe.wait_ge(ct_ready, b + 1)
                        pe.wait_ge(wo_split, NC)
                    last = halves(bank, lambda a, c: CT[:, b % 2, a, c, :], lambda a, c: WQ[:, a, c, 0:D], part)
                    done = wo_done
                else:
                    if part == 0:
                        pe.wait_ge(x1t_ready, b + 1)
                        pe.wait_ge(*freed(("WE", 0, NC - 1)))
                    last = halves(bank, lambda a, c: X1T[:, b % 2, a, c, :],
                                  lambda a, c: (WEL if a else WE)[:, c, :], part)
                    done = ffn_done
                if part == 2:
                    last.then_inc(done, 1)

            pe.wait_ge(consts, 1)
            for n in range(NJOB_A):
                for part in range(3):
                    pe_job(n, part)
                    for k in chunks_of_job(n, part):
                        chunk_scores(k)
                if n == ROWS0_AFTER:
                    turn_maxima(0)
            for job in JOBS[NJOB_A - RING:NJOB_A]:
                pe.wait_ge(*freed(job))
            pe.wait_ge(consts, 6)

            def filler(cyc, part):
                if cyc not in FILL:
                    return
                kind, b, _ = job = FILL[cyc]
                if job in JOB:
                    pe_job(JOB[job], part)
                else:
                    if part == 0:
                        misc_free(job)
                    pe_step(kind, b, MISC, part)

            def accumulate(cyc):
                u, kb = CYCLES[cyc]
                d = kb - TB * half_of(u)
                if d >= 0:
                    diag = sum(1 for v, k in CYCLES[:cyc + 1] if k >= TB * half_of(v))
                    pe.wait_ge(masked, 2 * diag)
                pe.wait_ge(probs, SCORE_BANKS[cyc + 1])
                d = max(d, 0)
                if kb == 0 and u:
                    pe.wait_ge(raw_out, u)
                n_kb = TB * (1 + half_of(u))
                for j in range(REP):
                    last = nc.tensor.matmul(PS[32 * j:32 * j + 32, PV_BANK, d * P:HT], VX[:, kb, u % G, :],
                                            PB[:, cyc % NP_BUF, j, d * P:HT], start=(kb == 0),
                                            stop=(kb == n_kb - 1))
                last.then_inc(pv_done, 1)

            def head_scores(cyc, j):
                u, kb = CYCLES[cyc]
                d = max(0, kb - TB * half_of(u))
                width = HT - d * P
                k, place = divmod(j, heads_per_bank(width))
                e = SCORE_BANKS[cyc] + k
                if place == 0:
                    if WIDE <= e < WIDE + MAX_BANKS:
                        pe.wait_ge(max_read, len(CHUNKS))
                    elif e >= WIDE + MAX_BANKS + ST_BANKS:
                        pe.wait_ge(probs, e - MAX_BANKS - ST_BANKS + 1)
                    elif e >= WIDE:
                        pe.wait_ge(probs, WIDE)
                    elif e >= ST_BANKS:
                        pe.wait_ge(probs, e - ST_BANKS + 1)
                last = nc.tensor.matmul(PS[:, score_bank(e), place * width:(place + 1) * width],
                                        KS[0:NROW, u % G, kb * P:(kb + 1) * P],
                                        QS[0:NROW, u % SLOTS, j, d * P:HT], start=True, stop=True)
                if place == heads_per_bank(width) - 1:
                    last.then_inc(scores, 1)

            for cyc, (u, kb) in enumerate(CYCLES):
                if kb == 0:
                    pe.wait_ge(nm_in, 16 * NPART * (u + 1))
                for j, lot in enumerate(chunks_of_cycle(cyc)):
                    for n in lot:
                        chunk_scores(n)
                    head_scores(cyc, j)
                    if j % 2:
                        filler(cyc, j // 2)
                if cyc:
                    accumulate(cyc - 1)
                filler(cyc, 2)
                if cyc in ROWS_AT:
                    turn_maxima(ROWS_AT[cyc])
            accumulate(NCYC - 1)

            pe.wait_ge(max_read, len(CHUNKS))
            pe.wait_ge(probs, SCORE_BANKS[NCYC])
            pe.wait_ge(*freed(MISC_ORDER[-1]))
            for kind, i in TAIL:
                b = B0 + i
                bank = tail_bank(kind, i)
                if kind == "T1":
                    for k, half in enumerate(("T1a", "T1b")):
                        if i >= 2:
                            pe.wait_ge(ctx_ready, 2 * (b - 2) + k + 1)
                        for part in range(3):
                            pe_step(half, b, bank + k, part)
                    continue
                if kind in ("T2", "T3") and i >= 2:
                    pe.wait_ge(*freed((kind, b - 2, 0)))
                if kind == "T3" and i < 2:
                    pe.wait_ge(*freed(("T2", b + 2, 0)))
                if kind == "WO" and i >= 2:
                    pe.wait_ge(*freed((kind, b - 2, 0)))
                if kind == "FF":
                    pe.wait_ge(ctx_ready, 2 * NT)
                for part in range(3):
                    pe_step(kind, b, bank, part)


_INS = ["L0_attn_x", "L0_attn_Wq", "L0_attn_Wkv", "L0_attn_Wo", "L0_attn_bo", "L0_ffn_lora_A", "L0_ffn_lora_B",
        "L0_ffn_W", "L0_ffn_bias", "L0_ffn_lora_weights"]
_OUTS = [((1, 1024, 512), "float32")]


def kernel(**inputs):
    import numpy as _np
    import concourse.bacc as _bacc
    from concourse import mybir as _mybir
    from concourse.bass_utils import run_bass_kernel_spmd as _run

    nc = _bacc.Bacc("TRN2", target_bir_lowering=False, num_devices=1)
    arrays, args = {}, []
    for name in _INS:
        a = _np.ascontiguousarray(inputs[name])
        arrays[f"in_{name}_dram"] = a
        args.append(nc.dram_tensor(f"in_{name}_dram", a.shape, _mybir.dt.from_np(a.dtype), kind="ExternalInput").ap())
    for i, (shape, dtype) in enumerate(_OUTS):
        dt = _mybir.dt.from_np(_np.dtype(dtype))
        args.append(nc.dram_tensor(f"out_{i}_dram", shape, dt, kind="ExternalOutput").ap())
    postln_kernel(nc, *args)
    r = _run(nc, [arrays], core_ids=[0])
    got = tuple(r.results[0][f"out_{i}_dram"] for i in range(len(_OUTS)))
    return got[0]
```
